# Optimizing a Trainium2 kernel written in Bass

```python
import numpy as np
import jax
import jax.numpy as jnp

def _softmax(x, axis=-1):
    return jax.nn.softmax(x, axis=axis)

def _gelu(x):
    return jax.nn.gelu(x, approximate=True)

def _silu(x):
    return jax.nn.silu(x)

def _sigmoid(x):
    return jax.nn.sigmoid(x)

def _layernorm(x, axis=-1, eps=1e-05):
    m = jnp.mean(x, axis=axis, keepdims=True)
    v = jnp.var(x, axis=axis, keepdims=True)
    return (x - m) / jnp.sqrt(v + eps)

def _scatter_add(tgt, idx, src, axis=0):
    return tgt.at[idx].add(src)

def _segment_sum(src, seg, n):
    return jax.ops.segment_sum(src, seg, n)
kernel_name = 'mk_gnn_preln_d2_gnn_r32_e49634'

def setup_inputs(seed: int=0):
    np.random.seed(seed)
    _w = jnp.asarray

    def _rec_inputs():
        import jax
        import jax.numpy as jnp
        _gk = jax.random.key(seed)
        x = -0.0008691 + 1 * jax.random.normal(jax.random.fold_in(_gk, 1), (50000, 128), jnp.float32)
        src = jax.random.randint(jax.random.fold_in(_gk, 2), (25000,), 0, 50000, jnp.int32)
        dst = jnp.minimum((50000 * jax.random.uniform(jax.random.fold_in(_gk, 3), (25000,)) ** 2.0).astype(jnp.int32), 49999)
        _o = jnp.argsort(dst, stable=True)
        src = src[_o]
        dst = dst[_o]
        edge_attr_64 = 0.000189758 + 1.00013 * jax.random.normal(jax.random.fold_in(_gk, 12), (25000, 64), jnp.float32)
        return (x, src, dst, edge_attr_64)
    x, src, dst, edge_attr_64 = _rec_inputs()

    def _L0_gnn_setup():
        import jax, jax.numpy as jnp
        import numpy as np
        N, C, E = (10000, 128, 20000)
        key = jax.random.key(seed)
        k1, k2, k3, k4 = jax.random.split(key, 4)
        x = jax.random.normal(k1, (N, C), dtype=jnp.float32)
        src = jax.random.randint(k2, (E,), 0, N)
        dst = jax.random.randint(k3, (E,), 0, N)
        W = jax.random.normal(k4, (2 * C, C), dtype=jnp.float32) / np.sqrt(2.0 * C)
        b = jnp.zeros((C,), dtype=jnp.float32)
        return {'x': x, 'W': W, 'b': b, 'src': src, 'dst': dst}
    _L0_gnn_all = _L0_gnn_setup()
    _L0_gnn_in = {k: v for k, v in _L0_gnn_all.items() if k in ('W', 'b')}
    del _L0_gnn_all

    def _L1_gnn_setup():
        import jax, jax.numpy as jnp
        import numpy as np
        N_NODES = 50000
        N_EDGES = 25000
        NODE_DIM = 128
        EDGE_DIM = 64
        HIDDEN = 128
        key = jax.random.key(seed)
        ks = jax.random.split(key, 12)
        s = lambda fan_in: 1.0 / np.sqrt(fan_in)
        inp = {'x': jax.random.normal(ks[0], (N_NODES, NODE_DIM), jnp.float32), 'edge_index': jax.random.randint(ks[1], (2, N_EDGES), 0, N_NODES, jnp.int32), 'edge_attr': jax.random.normal(ks[2], (N_EDGES, EDGE_DIM), jnp.float32), 'W_node': jax.random.uniform(ks[3], (NODE_DIM, HIDDEN), jnp.float32, -s(NODE_DIM), s(NODE_DIM)), 'b_node': jnp.zeros((HIDDEN,), jnp.float32), 'W_edge': jax.random.uniform(ks[4], (EDGE_DIM, HIDDEN), jnp.float32, -s(EDGE_DIM), s(EDGE_DIM)), 'b_edge': jnp.zeros((HIDDEN,), jnp.float32), 'W_att': jax.random.uniform(ks[5], (3 * HIDDEN, 1), jnp.float32, -s(3 * HIDDEN), s(3 * HIDDEN)), 'b_att': jnp.zeros((1,), jnp.float32), 'W_m1': jax.random.uniform(ks[6], (2 * NODE_DIM + EDGE_DIM, HIDDEN), jnp.float32, -s(2 * NODE_DIM + EDGE_DIM), s(2 * NODE_DIM + EDGE_DIM)), 'b_m1': jnp.zeros((HIDDEN,), jnp.float32), 'W_m2': jax.random.uniform(ks[7], (HIDDEN, HIDDEN), jnp.float32, -s(HIDDEN), s(HIDDEN)), 'b_m2': jnp.zeros((HIDDEN,), jnp.float32), 'W_m3': jax.random.uniform(ks[8], (HIDDEN, NODE_DIM), jnp.float32, -s(HIDDEN), s(HIDDEN)), 'b_m3': jnp.zeros((NODE_DIM,), jnp.float32)}
        return inp
    _L1_gnn_all = _L1_gnn_setup()
    _L1_gnn_in = {k: v for k, v in _L1_gnn_all.items() if k in ('W_node', 'b_node', 'W_edge', 'b_edge', 'W_att', 'b_att', 'W_m1', 'b_m1', 'W_m2', 'b_m2', 'W_m3', 'b_m3')}
    del _L1_gnn_all
    return {'x': x, 'src': src, 'dst': dst, 'edge_attr_64': edge_attr_64, 'L0_gnn_W': _L0_gnn_in['W'], 'L0_gnn_b': _L0_gnn_in['b'], 'L1_gnn_W_node': _L1_gnn_in['W_node'], 'L1_gnn_b_node': _L1_gnn_in['b_node'], 'L1_gnn_W_edge': _L1_gnn_in['W_edge'], 'L1_gnn_b_edge': _L1_gnn_in['b_edge'], 'L1_gnn_W_att': _L1_gnn_in['W_att'], 'L1_gnn_b_att': _L1_gnn_in['b_att'], 'L1_gnn_W_m1': _L1_gnn_in['W_m1'], 'L1_gnn_b_m1': _L1_gnn_in['b_m1'], 'L1_gnn_W_m2': _L1_gnn_in['W_m2'], 'L1_gnn_b_m2': _L1_gnn_in['b_m2'], 'L1_gnn_W_m3': _L1_gnn_in['W_m3'], 'L1_gnn_b_m3': _L1_gnn_in['b_m3']}

def reference(x, src, dst, edge_attr_64, L0_gnn_W, L0_gnn_b, L1_gnn_W_node, L1_gnn_b_node, L1_gnn_W_edge, L1_gnn_b_edge, L1_gnn_W_att, L1_gnn_b_att, L1_gnn_W_m1, L1_gnn_b_m1, L1_gnn_W_m2, L1_gnn_b_m2, L1_gnn_W_m3, L1_gnn_b_m3):
    import jax
    import jax.numpy as jnp

    def _L0_gnn_ref(x, W, b, src, dst):
        import jax, jax.numpy as jnp
        import numpy as np
        N, C, E = (10000, 128, 20000)
        xi = x[dst]
        xj = x[src]
        msg = jnp.concatenate([xi, xj - xi], axis=-1) @ W + b
        agg = jax.ops.segment_max(msg, dst, num_segments=x.shape[0])
        agg = jnp.where(jnp.isfinite(agg), agg, jnp.zeros_like(agg))
        return jax.nn.relu(agg)

    def _L1_gnn_ref(x, edge_index, edge_attr, W_node, b_node, W_edge, b_edge, W_att, b_att, W_m1, b_m1, W_m2, b_m2, W_m3, b_m3):
        import jax, jax.numpy as jnp
        import numpy as np
        N_NODES = 50000
        N_EDGES = 25000
        NODE_DIM = 128
        EDGE_DIM = 64
        HIDDEN = 128
        row, col = (edge_index[0], edge_index[1])
        x_proj = x @ W_node + b_node
        edge_proj = edge_attr @ W_edge + b_edge
        att_in = jnp.concatenate([x_proj[row], x_proj[col], edge_proj], axis=-1)
        alpha = att_in @ W_att + b_att
        alpha = jax.nn.softmax(alpha, axis=0)
        msg_in = jnp.concatenate([x[row], x[col], edge_attr], axis=-1)
        h = jax.nn.gelu(msg_in @ W_m1 + b_m1)
        h = jax.nn.gelu(h @ W_m2 + b_m2)
        messages = h @ W_m3 + b_m3
        weighted = alpha * messages
        out = jnp.zeros_like(x).at[col].add(weighted)
        return out
    edge_index = jnp.stack([src, dst])
    h = jnp.maximum(_layernorm(x, axis=-1), 0.0)
    x = x + _L0_gnn_ref(h, L0_gnn_W, L0_gnn_b, src, dst)
    h = jnp.maximum(_layernorm(x, axis=-1), 0.0)
    x = x + _L1_gnn_ref(h, edge_index, edge_attr_64, L1_gnn_W_node, L1_gnn_b_node, L1_gnn_W_edge, L1_gnn_b_edge, L1_gnn_W_att, L1_gnn_b_att, L1_gnn_W_m1, L1_gnn_b_m1, L1_gnn_W_m2, L1_gnn_b_m2, L1_gnn_W_m3, L1_gnn_b_m3)
    return x

_drawn_inputs = setup_inputs


def setup_inputs(seed=0):
    import zlib

    import numpy as np

    out = dict(_drawn_inputs(seed))
    spreads = {'L0_gnn_b': (0.0, 0.1),
     'L1_gnn_b_node': (0.0, 0.1),
     'L1_gnn_b_edge': (0.0, 0.1),
     'L1_gnn_b_m1': (0.0, 2.0),
     'L1_gnn_b_m2': (0.0, 2.0),
     'L1_gnn_b_m3': (0.0, 2.0)}
    factors = {'edge_attr_64': 8.0,
     'L1_gnn_W_node': 8.0,
     'L1_gnn_W_edge': 8.0,
     'L1_gnn_W_att': 8.0,
     'L1_gnn_W_m1': 8.0,
     'L1_gnn_W_m2': 8.0,
     'L1_gnn_W_m3': 8.0}
    for name, (base, spread) in spreads.items():
        noise = np.random.default_rng([zlib.crc32(name.encode()), seed]).standard_normal(out[name].shape)
        drawn = base * np.exp(spread * noise) if base else spread * noise
        out[name] = jnp.asarray(drawn.astype(out[name].dtype))
    for name, factor in factors.items():
        out[name] = (out[name] * factor).astype(out[name].dtype)
    return out
```

```python
from contextlib import ExitStack

import concourse.bass as bass
from concourse import mybir

F32 = mybir.dt.float32
I32 = mybir.dt.int32
U8 = mybir.dt.uint8
ALU = mybir.AluOpType
ACT = mybir.ActivationFunctionType
AX_X = mybir.AxisListType.X

P = 128
TPG = 4
GE = TPG * P
SLOTS = 4
EPS = 1e-5
SKIP = 1 << 20
LOWEST = -3.0e38
RSQRT_SEED = 0x5F3759DF


class Steps:

    def __init__(self, eng, sem):
        self.eng, self.sem, self.base, self.n = eng, sem, 0, 0

    def inc(self, ins):
        ins.then_inc(self.sem, 1)
        self.n += 1

    def wait(self):
        self.eng.wait_ge(self.sem, self.base + self.n)

    def enter(self, i, per_body):
        self.before, self.per_body = self.base + self.n, per_body
        self.base, self.n = self.before + i * per_body, 0

    def leave(self, trips):
        assert self.n == self.per_body, (self.n, self.per_body)
        self.base, self.n = self.before + trips * self.per_body, 0


def ago(g, d):
    k, u = g
    back = -((u - d) // SLOTS)
    return k - back, u - d + SLOTS * back


def over(eng, signal, g, each=1):
    k, u = g
    if isinstance(k, int) and k < 0:
        return
    if isinstance(signal, list):
        eng.wait_ge(signal[u], each * (k + 1))
    else:
        eng.wait_ge(signal, k * SLOTS + (u + 1))


def in_steps(eng, groups, deep, step, steps=None, per_step=0):
    first = deep + SLOTS
    first += (groups - first) % SLOTS
    trips = (groups - first) // SLOTS

    def peeled(m):
        step((m // SLOTS, m % SLOTS), lambda d: 0 <= m - d < groups)

    for m in range(first):
        peeled(m)
    with eng.Fori(0, trips) as i:
        if steps:
            steps.enter(i, SLOTS * per_step)
        for m in range(first, first + SLOTS):
            step((i + m // SLOTS, m % SLOTS), lambda d: True)
    if steps:
        steps.leave(trips)
    for m in range(groups, groups + deep):
        peeled(m)


def pipeline(eng, groups, stages, steps=None, per_step=0):
    def step(g, live):
        for lag, stage in stages:
            if live(lag):
                stage(ago(g, lag))

    in_steps(eng, groups, max(lag for lag, _ in stages), step, steps, per_step)


def gnn_kernel(nc, x, src, dst, edge_attr, W0, b0, W_node, b_node, W_edge, b_edge, W_att, b_att,
               W_m1, b_m1, W_m2, b_m2, W_m3, b_m3, out):
    N, C = x.shape
    E, DE = edge_attr.shape
    TILES = -(-E // GE) * TPG
    G = TILES // TPG
    EP = TILES * P
    HALF = TILES // 2
    TAIL = E - (TILES - 1) * P
    LAST = G - 1
    assert C == P and 0 < TAIL <= P and TILES % 2 == 0 and HALF <= P

    def number(g):
        return g[0] * SLOTS + g[1]

    def mirrored(g):
        return (LAST - g[1]) + g[0] * -SLOTS

    with ExitStack() as ctx:
        def sb(name, shape, dt=F32):
            return ctx.enter_context(nc.sbuf_tensor(name, shape, dt))

        def sem(name):
            return ctx.enter_context(nc.semaphore(name))

        def ring(name):
            return [sem(f"{name}{u}") for u in range(SLOTS)]

        def all_over(eng, signal, each=1):
            for n in range(G - SLOTS, G) if isinstance(signal, list) else (LAST,):
                over(eng, signal, (n // SLOTS, n % SLOTS), each)

        same_dram = nc.dram_tensor("same_dram", [1, EP + 1], U8).ap()
        mirror_dram = nc.dram_tensor("mirror_dram", [1, EP], U8).ap()
        y_dram = nc.dram_tensor("y_dram", [G, P, GE], F32).ap()
        part_dram = nc.dram_tensor("part_dram", [G, P, GE], F32).ap()
        logit_dst_dram = nc.dram_tensor("logit_dst_dram", [1, EP], F32).ap()
        logit_src_dram = nc.dram_tensor("logit_src_dram", [1, EP], F32).ap()

        ident = sb("ident", [P, P])
        flip = sb("flip", [HALF, HALF])
        ones = sb("ones", [P, P])
        w0_dst = sb("w0_dst", [P, P])
        w0_src = sb("w0_src", [P, P])
        w1_src = sb("w1_src", [P, P])
        w1_dst = sb("w1_dst", [P, P])
        w1_edge = sb("w1_edge", [DE + 1, P])
        w2 = sb("w2", [P, P])
        w3 = sb("w3", [P, P])
        wn = sb("wn", [P, P])
        we = sb("we", [DE, P])
        wnT = sb("wnT", [P, P])
        weT = sb("weT", [P, DE + 1])
        bnode_last = sb("bnode_last", [P, DE + 1])
        one_last = sb("one_last", [1, DE + 1])
        col = sb("col", [P, 3])
        watt = sb("watt", [P, 3])
        batt = sb("batt", [1, 1])
        u_src = sb("u_src", [P, 1])
        u_dst = sb("u_dst", [P, 1])
        u_edge = sb("u_edge", [DE + 1, 1])

        dst_row = sb("dst_row", [HALF, 2, P], I32)
        next_row = sb("next_row", [HALF, 2, P], I32)
        src_row = sb("src_row", [HALF, 2, P], I32)
        same_row = sb("same_row", [HALF, 2, P])
        mirror_row = sb("mirror_row", [HALF, 2, P])
        same_u8 = sb("same_u8", [HALF, 2, P], U8)
        mirror_u8 = sb("mirror_u8", [HALF, 2, P], U8)
        zero_u8 = sb("zero_u8", [1, 1], U8)
        idx_row = sb("idx_row", [HALF, 3, 2, P])
        idx = sb("idx", [P, G, 3 * TPG], I32)
        is_last = sb("is_last", [P, G, TPG])
        idx_now = sb("idx_now", [P, SLOTS, 3 * TPG], I32)

        big = sb("big", [P, EP])
        xs = sb("xs", [P, SLOTS, GE])
        xd = sb("xd", [P, SLOTS, GE])
        flags = sb("flags", [P, SLOTS, GE], U8)
        xn = sb("xn", [P, 2, 2 * GE])
        hs = sb("hs", [P, 2, GE])
        hd = sb("hd", [P, 2, GE])
        m_a = sb("m_a", [P, 2, GE])
        run = sb("run", [P, 2, GE])
        y_out = sb("y_out", [P, SLOTS, GE])
        ea = sb("ea", [P, SLOTS, TPG * DE])
        eaT = sb("eaT", [DE + 1, 2, GE])
        l_row = sb("l_row", [1, SLOTS, GE])
        lc = sb("lc", [P, 2, TILES])
        sm = sb("sm", [P, 8])
        mrow = sb("mrow", [1, 2])
        bst = sb("bst", [P, 2 * TPG, 6])
        mv = sb("mv", [P, 2, 2 * TPG, 2])
        var = sb("var", [P, 2 * TPG])
        half_bits = sb("half_bits", [P, 2 * TPG], I32)
        newton = sb("newton", [P, 2 * TPG])
        rstd = sb("rstd", [P, 2, 2 * TPG])

        bank = [ctx.enter_context(nc.psum_tensor(f"bank{i}", [P, 512], F32)) for i in range(8)]

        s_fill = sem("s_fill")
        s_index = sem("s_index")
        s_weights = sem("s_weights")
        s_zeroed = sem("s_zeroed")
        s_ident0 = sem("s_ident0")
        s_ident = sem("s_ident")
        s_ones = sem("s_ones")
        s_dve = sem("s_dve")
        s_link = sem("s_link")
        s_same = sem("s_same")
        s_rows = sem("s_rows")
        s_mirrored = sem("s_mirrored")
        s_mirror = sem("s_mirror")
        s_idx_rows = sem("s_idx_rows")
        s_idxT = sem("s_idxT")
        s_idx = sem("s_idx")
        s_flags_dram = sem("s_flags_dram")
        s_wdiff = sem("s_wdiff")
        s_wT = sem("s_wT")
        s_wT_in = sem("s_wT_in")
        s_u = sem("s_u")
        s_u_in = sem("s_u_in")
        s_eaT_ones = sem("s_eaT_ones")
        s_copy = sem("s_copy")
        s_taken = sem("s_taken")
        s_issue = sem("s_issue")
        a_flags = ring("a_flags")
        a_gathered = ring("a_gathered")
        a_copied = sem("a_copied")
        a_normed = sem("a_normed")
        a_turned = sem("a_turned")
        a_relu = sem("a_relu")
        a_msg = sem("a_msg")
        a_biased = sem("a_biased")
        a_max = sem("a_max")
        a_back = sem("a_back")
        a_y = sem("a_y")
        s_spilled = sem("s_spilled")
        s_staged = sem("s_staged")
        s_scattered = ring("s_scattered")
        s_flags = ring("s_flags")
        s_ea = ring("s_ea")
        s_ea_tail = sem("s_ea_tail")
        s_normed = sem("s_normed")
        s_turned = sem("s_turned")
        s_eaT = sem("s_eaT")
        s_hd = sem("s_hd")
        s_first = sem("s_first")
        s_part = sem("s_part")
        s_part_out = ring("s_part_out")
        s_run0 = sem("s_run0")
        b_gathered = ring("b_gathered")
        b_part = ring("b_part")
        b_normed = sem("b_normed")
        b_turned = sem("b_turned")
        b_hs = sem("b_hs")
        b_first = sem("b_first")
        b_sum = sem("b_sum")
        b_lrow = sem("b_lrow")
        b_lout = ring("b_lout")
        b_g1 = sem("b_g1")
        b_second = sem("b_second")
        b_g2 = sem("b_g2")
        b_third = sem("b_third")
        b_msg = sem("b_msg")
        s_lc0 = sem("s_lc0")
        s_lc = sem("s_lc")
        s_ladd = sem("s_ladd")
        s_max = sem("s_max")
        s_maxT = sem("s_maxT")
        s_max1 = sem("s_max1")
        s_maxb = sem("s_maxb")
        s_negmax = sem("s_negmax")
        s_exps = sem("s_exps")
        s_sum = sem("s_sum")
        s_inv = sem("s_inv")
        c_rows = ring("c_rows")
        c_flags = ring("c_flags")
        c_y = ring("c_y")
        c_logit = sem("c_logit")
        c_w = sem("c_w")
        c_wm = sem("c_wm")
        c_sum = sem("c_sum")
        c_back = sem("c_back")
        c_out = sem("c_out")
        c_scattered = ring("c_scattered")

        def flat(a):
            return a.rearrange("(o n) -> o n", o=1)

        def column(a):
            return a.rearrange("(n o) -> n o", o=1)

        def tile(buf, u, j, width=P):
            return buf[:, u, j * width:(j + 1) * width]

        def segment(n):
            return big[:, bass.ds(n * GE, GE)]

        def whole(dram, n):
            return dram[bass.ds(n, 1), :, :].rearrange("g p n -> p (g n)")

        block = ctx.enter_context(nc.Block())
        N_W = 19
        COPY_ROWS = N // 4 // 100
        A_GATHERS = 2 * TPG * 16
        GATHERS = TPG * 16

        @block.sync
        def _(sp):
            sp.wait_ge(s_fill, 3)
            for row, a, shift in ((dst_row, dst, 0), (next_row, dst, 1), (src_row, src, 0)):
                mid, end = HALF * P, (TILES - 1) * P
                sp.dma_start(row[:, 0, :], a[shift:mid + shift].rearrange("(t p) -> t p", p=P)
                             ).then_inc(s_index, 16)
                sp.dma_start(row[0:HALF - 1, 1, :], a[mid + shift:end + shift].rearrange("(t p) -> t p", p=P)
                             ).then_inc(s_index, 16)
                sp.dma_start(row[HALF - 1:HALF, 1, 0:TAIL - shift], flat(a[end + shift:E])).then_inc(s_index, 16)
            sp.wait_ge(s_same, 1)
            sp.dma_start(same_dram[:, 0:1], zero_u8[:, :]).then_inc(s_flags_dram, 16)
            for h in range(2):
                sp.dma_start(same_dram[0, 1 + h * HALF * P:1 + (h + 1) * HALF * P].rearrange("(t p) -> t p", p=P),
                             same_u8[:, h, :]).then_inc(s_flags_dram, 16)
            sp.wait_ge(s_mirror, 1)
            for h in range(2):
                sp.dma_start(mirror_dram[0, h * HALF * P:(h + 1) * HALF * P].rearrange("(t p) -> t p", p=P),
                             mirror_u8[:, h, :]).then_inc(s_flags_dram, 16)
            sp.wait_ge(s_flags_dram, 16 * 5)

            def flags_a(g):
                over(sp, a_max, ago(g, SLOTS))
                sp.dma_start(flags[:, g[1], :], same_dram[:, bass.ds(number(g) * GE, GE)].broadcast_to([P, GE])
                             ).then_inc(a_flags[g[1]], 16)

            def spill(g):
                over(sp, a_y, g)
                sp.dma_start(whole(y_dram, number(g)), segment(number(g))).then_inc(s_spilled, 16)

            pipeline(sp, G, [(0, flags_a), (7, spill)])

            full = TPG - 1
            sp.wait_ge(s_fill, 4)
            sp.dma_start(ea[0:TAIL, 0, full * DE:TPG * DE], edge_attr[E - TAIL:E, :]).then_inc(s_ea_tail, 16)

            def inputs_s(g):
                k, u = g
                over(sp, s_hd, ago(g, SLOTS))
                sp.dma_start(flags[:, u, :], mirror_dram[:, bass.ds(number(g) * GE, GE)].broadcast_to([P, GE])
                             ).then_inc(s_flags[u], 16)
                over(sp, s_turned, ago(g, SLOTS))
                n = mirrored(g)
                tiles = full if isinstance(n, int) and n == LAST else TPG
                sp.dma_start(ea[:, u, 0:tiles * DE].rearrange("p (j d) -> p j d", d=DE),
                             edge_attr[bass.ds(n * GE, tiles * P), :].rearrange("(j p) d -> p j d", p=P)
                             ).then_inc(s_ea[u], 16)

            def part_out(g):
                k, u = g
                over(sp, s_part, g)
                sp.dma_start(whole(part_dram, mirrored(g)), xs[:, u, :]).then_inc(s_part_out[u], 16)
                sp.dma_start(logit_dst_dram[:, bass.ds(mirrored(g) * GE, GE)], l_row[:, u, :]
                             ).then_inc(s_part_out[u], 16)

            all_over(sp, a_max)
            pipeline(sp, G, [(0, inputs_s), (6, part_out)])

            all_over(sp, s_part_out, 32)

            def part_in(g):
                over(sp, b_sum, ago(g, SLOTS))
                sp.dma_start(xd[:, g[1], :], whole(part_dram, number(g))).then_inc(b_part[g[1]], 16)

            def logits_out(g):
                over(sp, b_lrow, g)
                sp.dma_start(logit_src_dram[:, bass.ds(number(g) * GE, GE)], l_row[:, g[1], :]
                             ).then_inc(b_lout[g[1]], 16)

            pipeline(sp, G, [(0, part_in), (6, logits_out)])

            sp.wait_ge(s_lc0, 1)
            all_over(sp, b_lout, 16)
            rows, rest = E // TILES, E % TILES
            for q, dram in enumerate((logit_dst_dram, logit_src_dram)):
                sp.dma_start(lc[0:rows, q, :], dram[0, 0:rows * TILES].rearrange("(p t) -> p t", t=TILES)
                             ).then_inc(s_lc, 16)
                if rest:
                    sp.dma_start(lc[rows:rows + 1, q, 0:rest], dram[:, rows * TILES:E]).then_inc(s_lc, 16)

            sp.wait_ge(s_spilled, 16 * G)
            all_over(sp, b_normed)
            all_over(sp, b_sum)

            def rows_c(g):
                k, u = g
                over(sp, c_logit, ago(g, SLOTS))
                for buf, dram in ((l_row, logit_dst_dram), (xs, logit_src_dram)):
                    sp.dma_start(buf[0:1, u, :], dram[:, bass.ds(number(g) * GE, GE)]).then_inc(c_rows[u], 16)

            def flags_c(g):
                over(sp, c_sum, ago(g, SLOTS))
                sp.dma_start(flags[:, g[1], :], same_dram[:, bass.ds(number(g) * GE, GE)].broadcast_to([P, GE])
                             ).then_inc(c_flags[g[1]], 16)

            def rows_y_c(g):
                over(sp, c_out, ago(g, SLOTS))
                sp.dma_start(xd[:, g[1], :], whole(y_dram, number(g))).then_inc(c_y[g[1]], 16)

            pipeline(sp, G, [(1, flags_c), (0, rows_c), (3, rows_y_c)])

        @block.gpsimd
        def _(pool):
            taken = Steps(pool, s_taken)
            last_row = pool.to_reg(N - 1)
            pool.memset(dst_row[:, :, :], N).then_inc(s_fill, 1)
            pool.memset(next_row[:, :, :], N).then_inc(s_fill, 1)
            pool.memset(src_row[:, :, :], 0).then_inc(s_fill, 1)
            pool.memset(ident[:, :], 0.0)
            pool.memset(flip[:, :], 0.0).then_inc(s_ident0, 1)
            pool.wait_ge(s_ident0, 1)
            pool.affine_select(out=ident[:, :], in_=ident[:, :], compare_op=ALU.not_equal, fill=1.0, base=0,
                               pattern=[[-1, P]], channel_multiplier=1)
            pool.affine_select(out=flip[:, :], in_=flip[:, :], compare_op=ALU.not_equal, fill=1.0,
                               base=-(HALF - 1), pattern=[[1, HALF]], channel_multiplier=1).then_inc(s_ident, 1)
            pool.memset(weT[:, :], 0.0)
            pool.memset(bnode_last[:, :], 0.0).then_inc(s_zeroed, 1)
            pool.memset(ea[:, 0, :], 0.0).then_inc(s_fill, 1)
            pool.memset(lc[:, :, :], LOWEST / 4).then_inc(s_lc0, 1)

            def take(order):
                def stage(g):
                    taken.inc(pool.tensor_copy(idx_now[:, g[1], :].rearrange("p (g n) -> p g n", g=1),
                                               idx[:, bass.ds(order(g), 1), :]))
                return stage

            def issue(g):
                pool.sem_inc(s_issue, 1)

            def at(u, table, j):
                c = table * TPG + j
                return bass.IndirectOffsetOnAxis(ap=idx_now[:, u, c:c + 1], axis=0)

            def gather(u, buf, table, rows, done):
                for j in range(TPG):
                    pool.indirect_dma_start(tile(buf, u, j), None, rows, at(u, table, j),
                                            bounds_check=last_row, oob_is_err=False).then_inc(done[u], 16)

            def scatter(u, done):
                for j in range(TPG):
                    pool.indirect_dma_start(out, at(u, 2, j), tile(y_out, u, j), None,
                                            bounds_check=last_row, oob_is_err=False).then_inc(done[u], 16)

            pool.wait_ge(s_idx, 1)

            def take_a(g):
                over(pool, a_gathered, ago(g, SLOTS), A_GATHERS)
                take(number)(g)

            def gather_a(g):
                over(pool, a_normed, ago(g, SLOTS))
                over(pool, a_copied, ago(g, SLOTS))
                taken.wait()
                issue(g)
                gather(g[1], xs, 0, x, a_gathered)
                gather(g[1], xd, 1, x, a_gathered)

            pipeline(pool, G, [(0, take_a), (0, gather_a)], taken, 1)
            all_over(pool, a_gathered, A_GATHERS)

            pool.wait_ge(s_copy, 16 * 4)

            def take_s(g):
                over(pool, s_scattered, ago(g, SLOTS), GATHERS)
                take(mirrored)(g)

            def scatter_s(g):
                over(pool, s_staged, g)
                taken.wait()
                issue(g)
                scatter(g[1], s_scattered)

            pipeline(pool, G, [(0, take_s), (0, scatter_s)], taken, 1)

            all_over(pool, s_scattered, GATHERS)
            all_over(pool, s_part_out, 32)

            def take_b(g):
                over(pool, b_gathered, ago(g, SLOTS), GATHERS)
                take(number)(g)

            def gather_b(g):
                over(pool, b_normed, ago(g, SLOTS))
                taken.wait()
                issue(g)
                gather(g[1], xs, 0, out, b_gathered)

            pipeline(pool, G, [(0, take_b), (0, gather_b)], taken, 1)
            all_over(pool, b_gathered, GATHERS)

            def take_c(g):
                over(pool, c_scattered, ago(g, SLOTS), GATHERS)
                take(number)(g)

            def scatter_c(g):
                over(pool, c_out, g)
                taken.wait()
                issue(g)
                scatter(g[1], c_scattered)

            pipeline(pool, G, [(0, take_c), (0, scatter_c)], taken, 1)
            all_over(pool, c_scattered, GATHERS)

        @block.vector
        def _(dve):
            st = Steps(dve, s_dve)
            dve.memset(zero_u8[:, :], 0)
            dve.memset(one_last[:, :], 0.0)
            dve.memset(eaT[DE:DE + 1, :, :], 1.0).then_inc(s_eaT_ones, 1)
            dve.memset(ones[:, :], 1.0).then_inc(s_ones, 1)
            dve.memset(run[:, 1, GE - 1:GE], 0.0)
            dve.memset(hd[:, 1, 0:1], 0.0).then_inc(s_run0, 1)

            dve.wait_ge(s_index, 16 * 9)
            st.inc(dve.tensor_tensor(same_row[:, :, :], dst_row[:, :, :], next_row[:, :, :], ALU.is_equal))
            dve.tensor_copy(idx_row[:, 0, :, :], src_row[:, :, :])
            dve.tensor_scalar(idx_row[:, 1, :, :], dst_row[:, :, :], float(N - 1), None, ALU.min)
            st.wait()
            dve.scalar_tensor_tensor(out=idx_row[:, 2, :, :], in0=same_row[:, :, :], scalar=float(SKIP),
                                     in1=dst_row[:, :, :], op0=ALU.mult, op1=ALU.add).then_inc(s_idx_rows, 1)
            dve.tensor_copy(same_u8[:, :, :], same_row[:, :, :]).then_inc(s_same, 1)
            for h in range(2):
                ins = dve.tensor_copy(mirror_row[:, h, :], same_row[:, h, ::-1])
            ins.then_inc(s_mirrored, 1)
            dve.wait_ge(s_idxT, 1)
            for table in range(3):
                dve.tensor_copy(idx[:, :, table * TPG:(table + 1) * TPG],
                                bank[table][:, 0:TILES].rearrange("p (g j) -> p g j", j=TPG))
            dve.tensor_scalar(is_last[:, :, :], bank[2][:, 0:TILES].rearrange("p (g j) -> p g j", j=TPG),
                              float(SKIP), None, ALU.is_lt).then_inc(s_idx, 1)
            for h in range(2):
                ins = dve.tensor_copy(mirror_u8[:, 1 - h, :], bank[3][0:HALF, h * P:(h + 1) * P])
            ins.then_inc(s_mirror, 1)

            dve.wait_ge(s_weights, 16 * N_W)
            dve.wait_ge(s_eaT_ones, 1)
            dve.memset(one_last[:, DE:DE + 1], 1.0)
            dve.tensor_tensor(w0_dst[:, :], w0_dst[:, :], w0_src[:, :], ALU.subtract).then_inc(s_wdiff, 1)
            dve.wait_ge(s_wT, 1)
            dve.tensor_copy(wnT[:, :], bank[4][:, 0:P])
            dve.tensor_copy(weT[:, 0:DE], bank[5][:, 0:DE]).then_inc(s_wT_in, 1)
            dve.wait_ge(s_u, 1)
            dve.tensor_copy(u_src[:, :], bank[6][:, 0:1])
            dve.tensor_copy(u_dst[:, :], bank[6][:, 1:2])
            dve.tensor_copy(u_edge[:, :], bank[7][0:DE + 1, 0:1]).then_inc(s_u_in, 1)

            LN_STEPS = 14

            def norm_links(g, tiles, mask=None):
                m, d = len(tiles), g[1] % 2
                n0 = st.n
                for j, t in enumerate(tiles):
                    ins = dve.bn_stats(bst[:, j, :], t)
                st.inc(ins)
                yield
                st.wait()
                dve.sem_inc(s_link, 1)
                for j in range(m):
                    ins = dve.bn_aggr(mv[:, d, j, :], bst[:, j, :])
                st.inc(ins)
                yield
                v, y, t, h = var[:, 0:m], rstd[:, d, 0:m], newton[:, 0:m], half_bits[:, 0:m]
                st.wait()
                st.inc(dve.tensor_scalar(v, mv[:, d, 0:m, 1], EPS, None, ALU.add))
                yield
                st.wait()
                st.inc(dve.tensor_scalar(h, v.bitcast(I32), 1, None, ALU.logical_shift_right))
                yield
                st.wait()
                st.inc(dve.tensor_scalar(y.bitcast(I32), h, -1.0, float(RSQRT_SEED), ALU.mult, ALU.add))
                yield
                for step in range(3):
                    st.wait()
                    st.inc(dve.scalar_tensor_tensor(out=t, in0=y, scalar=-0.5, in1=y, op0=ALU.mult,
                                                    op1=ALU.mult))
                    yield
                    st.wait()
                    if step == 2 and mask is not None:
                        dve.tensor_tensor(y, y, mask, ALU.mult)
                    st.inc(dve.tensor_tensor(t, t, v, ALU.mult))
                    yield
                    st.wait()
                    st.inc(dve.scalar_tensor_tensor(out=y, in0=t, scalar=1.5, in1=y, op0=ALU.add, op1=ALU.mult))
                    yield
                assert st.n - n0 == LN_STEPS, st.n - n0

            def apply(g, tiles, j, done):
                d = g[1] % 2
                ins = dve.tensor_scalar(tile(xn, d, j), tiles[j], mv[:, d, j, 0:1], rstd[:, d, j:j + 1],
                                        ALU.subtract, ALU.mult)
                if j == len(tiles) - 1:
                    ins.then_inc(done, 1)

            def tiles_a(g):
                return [tile(buf, g[1], j) for buf in (xs, xd) for j in range(TPG)]

            def max_a(g):
                u, d = g[1], g[1] % 2
                over(dve, a_biased, g)
                over(dve, a_flags, g, 16)
                over(dve, a_back, ago(g, 2))
                over(dve, a_max, ago(g, 1))
                dve.tensor_tensor_scan(run[:, d, :], flags[:, u, :], m_a[:, d, :], run[:, 1 - d, GE - 1:GE],
                                       ALU.mult, ALU.max).then_inc(a_max, 1)

            def add_y(g):
                over(dve, a_back, g)
                over(dve, a_copied, g)
                dve.tensor_tensor(segment(number(g)), bank[6 + g[1] % 2][:, :], segment(number(g)), ALU.add
                                  ).then_inc(a_y, 1)

            def step_a(g, live):
                st.wait()
                if live(0):
                    over(dve, a_gathered, g, A_GATHERS)
                    chain = norm_links(g, tiles_a(g))
                else:
                    chain = iter(())
                next(chain, None)
                next(chain, None)
                if live(1):
                    over(dve, a_turned, ago(g, 3))
                    for j in range(2 * TPG):
                        apply(ago(g, 1), tiles_a(ago(g, 1)), j, a_normed)
                        next(chain, None)
                if live(3):
                    max_a(ago(g, 3))
                next(chain, None)
                if live(4):
                    add_y(ago(g, 4))
                for _ in chain:
                    pass

            dve.wait_ge(s_run0, 1)
            in_steps(dve, G, 4, step_a, st, LN_STEPS)

            def tiles_s(g):
                return [big[:, bass.ds(mirrored(g) * GE + j * P, P)] for j in range(TPG)]

            def spread_s(g):
                u, d = g[1], g[1] % 2
                over(dve, s_turned, g)
                over(dve, s_flags, g, 16)
                over(dve, s_first, ago(g, 2))
                over(dve, s_hd, ago(g, 1))
                dve.tensor_tensor_scan(hd[:, d, ::-1], flags[:, u, :], bank[d][:, ::-1],
                                       hd[:, 1 - d, 0:1], ALU.mult, ALU.max).then_inc(s_hd, 1)

            def step_s(g, live):
                st.wait()
                chain = iter(())
                if live(0):
                    chain = norm_links(g, tiles_s(g), is_last[:, bass.ds(mirrored(g), 1), :]
                                       .rearrange("p g j -> p (g j)"))
                next(chain, None)
                next(chain, None)
                if live(1):
                    over(dve, s_turned, ago(g, 3))
                    for j in range(TPG):
                        apply(ago(g, 1), tiles_s(ago(g, 1)), j, s_normed)
                        next(chain, None)
                if live(2):
                    spread_s(ago(g, 2))
                for _ in chain:
                    pass

            all_over(dve, a_y)
            all_over(dve, a_msg)
            dve.memset(hd[:, 1, 0:1], 0.0).then_inc(s_run0, 1)
            dve.wait_ge(s_run0, 2)
            in_steps(dve, G, 2, step_s, st, LN_STEPS)

            def tiles_b(g):
                return [tile(xs, g[1], j) for j in range(TPG)]

            def sum_b(g):
                u, d = g[1], g[1] % 2
                over(dve, b_first, g)
                over(dve, b_part, g, 16)
                over(dve, b_g1, ago(g, 2))
                dve.tensor_tensor(hd[:, d, :], bank[2 + d][:, :], xd[:, u, :], ALU.add).then_inc(b_sum, 1)

            def step_b(g, live):
                st.wait()
                chain = iter(())
                if live(0):
                    over(dve, b_gathered, g, GATHERS)
                    chain = norm_links(g, tiles_b(g))
                next(chain, None)
                next(chain, None)
                if live(1):
                    over(dve, b_turned, ago(g, 3))
                    for j in range(TPG):
                        apply(ago(g, 1), tiles_b(ago(g, 1)), j, b_normed)
                        next(chain, None)
                if live(3):
                    sum_b(ago(g, 3))
                for _ in chain:
                    pass

            all_over(dve, s_first)
            in_steps(dve, G, 3, step_b, st, LN_STEPS)

            dve.wait_ge(s_lc, 16 * 4)
            dve.tensor_tensor(lc[:, 0, :], lc[:, 0, :], lc[:, 1, :], ALU.add).then_inc(s_ladd, 1)
            dve.wait_ge(s_ladd, 1)
            dve.tensor_reduce(sm[:, 0:1], lc[:, 0, :], AX_X, ALU.max).then_inc(s_max, 1)
            dve.wait_ge(s_maxT, 1)
            dve.tensor_reduce(mrow[:, 0:1], bank[2][0:1, 0:P], AX_X, ALU.max).then_inc(s_max1, 1)
            dve.wait_ge(s_maxb, 1)
            dve.tensor_scalar(sm[:, 1:2], bank[3][:, 0:1], -1.0, None, ALU.mult).then_inc(s_negmax, 1)
            dve.wait_ge(s_sum, 1)
            dve.reciprocal(sm[:, 3:4], bank[4][:, 0:1]).then_inc(s_inv, 1)
            all_over(dve, b_third)
            dve.memset(run[:, 1, GE - 1:GE], 0.0).then_inc(s_inv, 1)
            dve.wait_ge(s_inv, 2)

            def weigh(g):
                u, d = g[1], g[1] % 2
                over(dve, c_w, g)
                over(dve, c_sum, ago(g, 2))
                dve.scalar_tensor_tensor(out=hd[:, d, :], in0=segment(number(g)), scalar=sm[:, 3:4],
                                         in1=m_a[:, d, :], op0=ALU.mult, op1=ALU.mult).then_inc(c_wm, 1)

            def sum_c(g):
                u, d = g[1], g[1] % 2
                over(dve, c_wm, g)
                over(dve, c_flags, g, 16)
                over(dve, c_back, ago(g, 2))
                over(dve, c_sum, ago(g, 1))
                dve.tensor_tensor_scan(run[:, d, :], flags[:, u, :], hd[:, d, :], run[:, 1 - d, GE - 1:GE],
                                       ALU.mult, ALU.add).then_inc(c_sum, 1)

            def add_out(g):
                u, d = g[1], g[1] % 2
                over(dve, c_back, g)
                over(dve, c_y, g, 16)
                over(dve, c_scattered, ago(g, SLOTS), GATHERS)
                dve.tensor_tensor(y_out[:, u, :], bank[6 + d][:, :], xd[:, u, :], ALU.add).then_inc(c_out, 1)

            all_over(dve, b_msg)
            pipeline(dve, G, [(2, weigh), (3, sum_c), (5, add_out)])

        @block.tensor
        def _(pe):
            def turn(dest, source, rows=P):
                for j in range(TPG):
                    ins = pe.transpose(dest[0:rows, j * P:(j + 1) * P], source(j), ident[:, :])
                return ins

            pe.wait_ge(s_ident, 1)
            pe.wait_ge(s_idx_rows, 1)
            for table in range(3):
                for h in range(2):
                    ins = pe.transpose(bank[table][:, h * HALF:(h + 1) * HALF], idx_row[:, table, h, :],
                                       ident[0:HALF, 0:HALF])
            pe.wait_ge(s_mirrored, 1)
            for h in range(2):
                ins = pe.matmul(bank[3][0:HALF, h * P:(h + 1) * P], flip[:, :], mirror_row[:, h, :],
                                start=True, stop=True)
            ins.then_inc(s_idxT, 1)
            pe.wait_ge(s_weights, 16 * N_W)
            pe.transpose(bank[4][:, 0:P], wn[:, :], ident[:, :])
            pe.transpose(bank[5][:, 0:DE], we[:, :], ident[0:DE, 0:DE]).then_inc(s_wT, 1)
            pe.wait_ge(s_wdiff, 1)
            pe.wait_ge(s_wT_in, 1)
            pe.matmul(bank[6][:, 0:1], wnT[:, :], watt[:, 0:1], start=True, stop=True)
            pe.matmul(bank[6][:, 1:2], wnT[:, :], watt[:, 1:2], start=True, stop=True)
            const = bank[7][0:DE + 1, 0:1]
            pe.matmul(const, weT[:, :], watt[:, 2:3], start=True, stop=False)
            pe.matmul(const, bnode_last[:, :], watt[:, 0:1], start=False, stop=False)
            pe.matmul(const, bnode_last[:, :], watt[:, 1:2], start=False, stop=False)
            pe.matmul(const, one_last[:, :], batt[:, :], start=False, stop=True).then_inc(s_u, 1)
            pe.wait_ge(s_u_in, 1)

            def turn_a(g):
                d = g[1] % 2
                over(pe, a_normed, g)
                over(pe, a_relu, ago(g, 2))
                turn(bank[d], lambda j: tile(xn, d, j))
                turn(bank[2 + d], lambda j: tile(xn, d, TPG + j)).then_inc(a_turned, 1)

            def messages_a(g):
                d = g[1] % 2
                over(pe, a_relu, g)
                over(pe, a_biased, ago(g, 2))
                pe.matmul(bank[4 + d][:, :], w0_src[:, :], hs[:, d, :], start=True, stop=False)
                pe.matmul(bank[4 + d][:, :], w0_dst[:, :], hd[:, d, :], start=False, stop=True
                          ).then_inc(a_msg, 1)

            def back_a(g):
                d = g[1] % 2
                over(pe, a_max, g)
                over(pe, a_y, ago(g, 2))
                turn(bank[6 + d], lambda j: tile(run, d, j)).then_inc(a_back, 1)

            pipeline(pe, G, [(1, turn_a), (2, messages_a), (3, back_a)])

            def turn_s(g):
                u, d = g[1], g[1] % 2
                over(pe, s_normed, g)
                over(pe, s_ea, g, 16)
                over(pe, s_hd, ago(g, 2))
                over(pe, s_eaT, ago(g, 2))
                turn(bank[d], lambda j: tile(xn, d, j))
                turn(bank[2 + d], lambda j: tile(ea, u, j, DE), DE).then_inc(s_turned, 1)

            def first_s(g):
                u, d = g[1], g[1] % 2
                over(pe, s_hd, g)
                over(pe, s_eaT, g)
                over(pe, s_part, ago(g, 2))
                for dest, w_d, w_e in ((bank[4 + d][:, :], w1_dst, w1_edge),
                                       (bank[6 + d][0:1, :], u_dst, u_edge)):
                    pe.matmul(dest, w_e[:, :], eaT[:, d, :], start=True, stop=False)
                    ins = pe.matmul(dest, w_d[:, :], hd[:, d, :], start=False, stop=True)
                ins.then_inc(s_first, 1)

            all_over(pe, a_y)
            pe.wait_ge(s_ea_tail, 16)
            pipeline(pe, G, [(1, turn_s), (3, first_s)])

            def turn_b(g):
                d = g[1] % 2
                over(pe, b_normed, g)
                over(pe, b_hs, ago(g, 2))
                turn(bank[d], lambda j: tile(xn, d, j)).then_inc(b_turned, 1)

            def first_b(g):
                d = g[1] % 2
                over(pe, b_hs, g)
                over(pe, b_sum, ago(g, 2))
                over(pe, b_lrow, ago(g, 2))
                pe.matmul(bank[2 + d][:, :], w1_src[:, :], hs[:, d, :], start=True, stop=True)
                pe.matmul(bank[4 + d][0:1, :], u_src[:, :], hs[:, d, :], start=True, stop=True
                          ).then_inc(b_first, 1)

            def second_b(g):
                over(pe, b_g1, g)
                over(pe, b_g2, ago(g, 1))
                pe.matmul(bank[6][:, :], w2[:, :], m_a[:, g[1] % 2, :], start=True, stop=True
                          ).then_inc(b_second, 1)

            def third_b(g):
                over(pe, b_g2, g)
                over(pe, b_msg, ago(g, 1))
                pe.matmul(bank[7][:, :], w3[:, :], run[:, g[1] % 2, :], start=True, stop=True
                          ).then_inc(b_third, 1)

            all_over(pe, s_part)
            pipeline(pe, G, [(1, turn_b), (2, first_b), (5, second_b), (6, third_b)])

            pe.wait_ge(s_max, 1)
            all_over(pe, b_sum)
            all_over(pe, b_lrow)
            pe.transpose(bank[2][0:1, 0:P], sm[:, 0:1], ident[:, :]).then_inc(s_maxT, 1)
            pe.wait_ge(s_max1, 1)
            pe.matmul(bank[3][:, 0:1], ones[0:1, :], mrow[:, 0:1], start=True, stop=True).then_inc(s_maxb, 1)
            pe.wait_ge(s_exps, 1)
            pe.matmul(bank[4][:, 0:1], ones[:, :], sm[:, 2:3], start=True, stop=True).then_inc(s_sum, 1)

            def logits_c(g):
                u, d = g[1], g[1] % 2
                over(pe, c_rows, g, 32)
                over(pe, c_w, ago(g, 2))
                pe.matmul(bank[d][:, :], ones[0:1, :], l_row[:, u, :], start=True, stop=False)
                pe.matmul(bank[d][:, :], ones[0:1, :], xs[0:1, u, :], start=False, stop=True
                          ).then_inc(c_logit, 1)

            def back_c(g):
                d = g[1] % 2
                over(pe, c_sum, g)
                over(pe, c_out, ago(g, 2))
                turn(bank[6 + d], lambda j: tile(run, d, j)).then_inc(c_back, 1)

            all_over(pe, b_msg)
            pipeline(pe, G, [(0, logits_c), (4, back_c)])

        @block.scalar
        def _(act):
            for dest, a in ((w0_dst[:, :], W0[0:C, :]), (w0_src[:, :], W0[C:2 * C, :]),
                            (w1_src[:, :], W_m1[0:C, :]), (w1_dst[:, :], W_m1[C:2 * C, :]),
                            (w1_edge[0:DE, :], W_m1[2 * C:2 * C + DE, :]), (w1_edge[DE:DE + 1, :], flat(b_m1)),
                            (w2[:, :], W_m2), (w3[:, :], W_m3), (wn[:, :], W_node), (we[:, :], W_edge),
                            (col[:, 0:1], column(b0)), (col[:, 1:2], column(b_m2)), (col[:, 2:3], column(b_m3)),
                            (watt[:, 0:1], W_att[0:P, :]), (watt[:, 1:2], W_att[P:2 * P, :]),
                            (watt[:, 2:3], W_att[2 * P:3 * P, :]), (batt[:, :], flat(b_att))):
                act.dma_start(dest, a).then_inc(s_weights, 16)
            act.wait_ge(s_zeroed, 1)
            act.dma_start(bnode_last[:, DE:DE + 1], column(b_node)).then_inc(s_weights, 16)
            act.dma_start(weT[:, DE:DE + 1], column(b_edge)).then_inc(s_weights, 16)
            for q in range(4):
                n0, n1 = q * N // 4, (q + 1) * N // 4
                act.dma_start(out[n0:n1, :].rearrange("(a b) c -> a (b c)", b=COPY_ROWS),
                              x[n0:n1, :].rearrange("(a b) c -> a (b c)", b=COPY_ROWS)).then_inc(s_copy, 16)

            def copy_a(g):
                over(act, a_gathered, g, A_GATHERS)
                act.activation(segment(number(g)), xd[:, g[1], :], ACT.Copy).then_inc(a_copied, 1)

            def relu_a(g):
                d = g[1] % 2
                over(act, a_turned, g)
                over(act, a_msg, ago(g, 2))
                act.activation(hs[:, d, :], bank[d][:, :], ACT.Relu)
                act.activation(hd[:, d, :], bank[2 + d][:, :], ACT.Relu).then_inc(a_relu, 1)

            def bias_a(g):
                d = g[1] % 2
                over(act, a_msg, g)
                over(act, a_max, ago(g, 2))
                act.activation(m_a[:, d, :], bank[4 + d][:, :], ACT.Identity, bias=col[:, 0:1]
                               ).then_inc(a_biased, 1)

            act.wait_ge(s_weights, 16 * N_W)
            act.wait_ge(s_run0, 1)
            pipeline(act, G, [(0, copy_a), (1, relu_a), (2, bias_a)])

            def stage_s(g):
                over(act, s_scattered, ago(g, SLOTS), GATHERS)
                act.activation(y_out[:, g[1], :], segment(mirrored(g)), ACT.Copy).then_inc(s_staged, 1)

            def edge_s(g):
                d = g[1] % 2
                over(act, s_turned, g)
                over(act, s_first, ago(g, 2))
                act.activation(eaT[0:DE, d, :], bank[2 + d][0:DE, :], ACT.Copy).then_inc(s_eaT, 1)

            def part_s(g):
                u, d = g[1], g[1] % 2
                over(act, s_first, g)
                over(act, s_part_out, ago(g, SLOTS), 32)
                act.activation(xs[:, u, :], bank[4 + d][:, :], ACT.Copy)
                act.activation(l_row[:, u, :], bank[6 + d][0:1, :], ACT.Copy).then_inc(s_part, 1)

            all_over(act, a_y)
            pipeline(act, G, [(0, stage_s), (2, edge_s), (4, part_s)])

            def relu_b(g):
                d = g[1] % 2
                over(act, b_turned, g)
                over(act, b_first, ago(g, 2))
                act.activation(hs[:, d, :], bank[d][:, :], ACT.Relu).then_inc(b_hs, 1)

            def logits_b(g):
                u, d = g[1], g[1] % 2
                over(act, b_first, g)
                over(act, b_lout, ago(g, SLOTS), 16)
                act.activation(l_row[:, u, :], bank[4 + d][0:1, :], ACT.Copy).then_inc(b_lrow, 1)

            def gelu1_b(g):
                d = g[1] % 2
                over(act, b_sum, g)
                over(act, b_second, ago(g, 2))
                act.activation(m_a[:, d, :], hd[:, d, :], ACT.Gelu_apprx_tanh).then_inc(b_g1, 1)

            def gelu2_b(g):
                d = g[1] % 2
                over(act, b_second, g)
                over(act, b_third, ago(g, 2))
                act.activation(run[:, d, :], bank[6][:, :], ACT.Gelu_apprx_tanh, bias=col[:, 1:2]
                               ).then_inc(b_g2, 1)

            def message_b(g):
                over(act, b_third, g)
                act.activation(segment(number(g)), bank[7][:, :], ACT.Identity, bias=col[:, 2:3]
                               ).then_inc(b_msg, 1)

            all_over(act, s_staged)
            all_over(act, s_normed)
            all_over(act, s_part_out, 32)
            act.wait_ge(s_spilled, 16 * G)
            pipeline(act, G, [(1, relu_b), (3, logits_b), (4, gelu1_b), (5, gelu2_b), (6, message_b)])

            act.wait_ge(s_negmax, 1)
            act.activation(lc[:, 1, :], lc[:, 0, :], ACT.Exp, bias=sm[:, 1:2], accum_out=sm[:, 2:3]
                           ).then_inc(s_exps, 1)

            def weights_c(g):
                d = g[1] % 2
                over(act, c_logit, g)
                over(act, c_wm, ago(g, 2))
                act.activation(m_a[:, d, :], bank[d][:, :], ACT.Exp, bias=sm[:, 1:2]).then_inc(c_w, 1)

            pipeline(act, G, [(1, weights_c)])

_INS = ['x', 'src', 'dst', 'edge_attr_64', 'L0_gnn_W', 'L0_gnn_b', 'L1_gnn_W_node', 'L1_gnn_b_node',
        'L1_gnn_W_edge', 'L1_gnn_b_edge', 'L1_gnn_W_att', 'L1_gnn_b_att', 'L1_gnn_W_m1', 'L1_gnn_b_m1',
        'L1_gnn_W_m2', 'L1_gnn_b_m2', 'L1_gnn_W_m3', 'L1_gnn_b_m3']


def kernel(**inputs):
    import numpy as _np
    import concourse.bacc as _bacc
    from concourse import mybir as _mybir
    from concourse.bass_utils import run_bass_kernel_spmd as _run

    nc = _bacc.Bacc("TRN2", target_bir_lowering=False, num_devices=1)
    arrays, args = {}, []
    for name in _INS:
        a = _np.ascontiguousarray(inputs[name])
        arrays[f"in_{name}_dram"] = a
        args.append(nc.dram_tensor(f"in_{name}_dram", a.shape, _mybir.dt.from_np(a.dtype), kind="ExternalInput").ap())
    shape = tuple(inputs["x"].shape)
    out = nc.dram_tensor("out_0_dram", shape, _mybir.dt.float32, kind="ExternalOutput").ap()
    gnn_kernel(nc, *args, out)
    r = _run(nc, [arrays], core_ids=[0])
    return r.results[0]["out_0_dram"]
```

```python
from contextlib import ExitStack

import concourse.bass as bass
from concourse import mybir

F32 = mybir.dt.float32
I32 = mybir.dt.int32
U8 = mybir.dt.uint8
ALU = mybir.AluOpType
ACT = mybir.ActivationFunctionType
AX_X = mybir.AxisListType.X

P = 128
TPG = 4
GE = TPG * P
SLOTS = 4
EPS = 1e-5
SKIP = 1 << 20
LOWEST = -3.0e38
RSQRT_SEED = 0x5F3759DF


class Steps:

    def __init__(self, eng, sem):
        self.eng, self.sem, self.base, self.n = eng, sem, 0, 0

    def inc(self, ins):
        ins.then_inc(self.sem, 1)
        self.n += 1

    def wait(self, later=0):
        self.eng.wait_ge(self.sem, self.base + (self.n - later))

    def enter(self, i, per_body):
        self.before, self.per_body = self.base + self.n, per_body
        self.base, self.n = self.before + i * per_body, 0

    def leave(self, trips):
        assert self.n == self.per_body, (self.n, self.per_body)
        self.base, self.n = self.before + trips * self.per_body, 0


def ago(g, d):
    k, u = g
    back = -((u - d) // SLOTS)
    return k - back, u - d + SLOTS * back


def over(eng, signal, g, each=1):
    k, u = g
    if isinstance(k, int) and k < 0:
        return
    if isinstance(signal, list):
        eng.wait_ge(signal[u], each * (k + 1))
    else:
        eng.wait_ge(signal, k * SLOTS + (u + 1))


def in_steps(eng, groups, deep, step, steps=None, per_loop=0, ahead=0, before_drain=None):
    first = deep + SLOTS
    first += (groups - ahead - first) % SLOTS
    trips = (groups - ahead - first) // SLOTS

    def peeled(m):
        step((m // SLOTS, m % SLOTS), lambda d: 0 <= m - d < groups)

    for m in range(first):
        peeled(m)
    with eng.Fori(0, trips) as i:
        if steps:
            steps.enter(i, per_loop)
        for m in range(first, first + SLOTS):
            step((i + m // SLOTS, m % SLOTS), lambda d: True)
    if steps:
        steps.leave(trips)
    for m in range(groups - ahead, groups + deep):
        if m == groups and before_drain:
            before_drain()
        peeled(m)


def pipeline(eng, groups, stages, steps=None, per_loop=0, before_drain=None):
    def step(g, live):
        for lag, stage in stages:
            if live(lag):
                stage(ago(g, lag))

    in_steps(eng, groups, max(lag for lag, _ in stages), step, steps, per_loop,
             max(0, -min(lag for lag, _ in stages)), before_drain)


def gnn_kernel(nc, x, src, dst, edge_attr, W0, b0, W_node, b_node, W_edge, b_edge, W_att, b_att,
               W_m1, b_m1, W_m2, b_m2, W_m3, b_m3, out):
    N, C = x.shape
    E, DE = edge_attr.shape
    TILES = -(-E // GE) * TPG
    G = TILES // TPG
    EP = TILES * P
    HALF = TILES // 2
    TAIL = E - (TILES - 1) * P
    LAST = G - 1
    assert C == P and 0 < TAIL <= P and TILES % 2 == 0 and HALF <= P

    def number(g):
        return g[0] * SLOTS + g[1]

    def mirrored(g):
        return (LAST - g[1]) + g[0] * -SLOTS

    with ExitStack() as ctx:
        def sb(name, shape, dt=F32):
            return ctx.enter_context(nc.sbuf_tensor(name, shape, dt))

        def sem(name):
            return ctx.enter_context(nc.semaphore(name))

        def ring(name):
            return [sem(f"{name}{u}") for u in range(SLOTS)]

        def all_over(eng, signal, each=1):
            for n in range(G - SLOTS, G) if isinstance(signal, list) else (LAST,):
                over(eng, signal, (n // SLOTS, n % SLOTS), each)

        same_dram = nc.dram_tensor("same_dram", [1, EP + 1], U8).ap()
        mirror_dram = nc.dram_tensor("mirror_dram", [1, EP], U8).ap()
        y_dram = nc.dram_tensor("y_dram", [G, P, GE], F32).ap()
        logit_dst_dram = nc.dram_tensor("logit_dst_dram", [1, EP], F32).ap()
        logit_src_dram = nc.dram_tensor("logit_src_dram", [1, EP], F32).ap()
        part_dram = nc.dram_tensor("part_dram", [G, P, GE], F32).ap()

        ident = sb("ident", [P, P])
        flip = sb("flip", [HALF, HALF])
        ones = sb("ones", [P, P])
        w0_dst = sb("w0_dst", [P, P])
        w0_src = sb("w0_src", [P, P])
        w1_src = sb("w1_src", [P, P])
        w1_dst = sb("w1_dst", [P, P])
        w1_edge = sb("w1_edge", [DE + 1, P])
        w2 = sb("w2", [P, P])
        w3 = sb("w3", [P, P])
        wn = sb("wn", [P, P])
        we = sb("we", [DE, P])
        wnT = sb("wnT", [P, P])
        weT = sb("weT", [P, DE + 1])
        bnode_last = sb("bnode_last", [P, DE + 1])
        one_last = sb("one_last", [1, DE + 1])
        col = sb("col", [P, 3])
        watt = sb("watt", [P, 3])
        batt = sb("batt", [1, 1])
        u_src = sb("u_src", [P, 1])
        u_dst = sb("u_dst", [P, 1])
        u_edge = sb("u_edge", [DE + 1, 1])

        dst_row = sb("dst_row", [HALF, 2, P], I32)
        next_row = sb("next_row", [HALF, 2, P], I32)
        src_row = sb("src_row", [HALF, 2, P], I32)
        same_row = sb("same_row", [HALF, 2, P])
        mirror_row = sb("mirror_row", [HALF, 2, P])
        same_u8 = sb("same_u8", [HALF, 2, P], U8)
        mirror_u8 = sb("mirror_u8", [HALF, 2, P], U8)
        zero_u8 = sb("zero_u8", [1, 1], U8)
        idx_row = sb("idx_row", [HALF, 3, 2, P])
        idx = sb("idx", [P, G + 1, 3 * TPG], I32)
        is_last = sb("is_last", [P, G, TPG])
        idx_now = sb("idx_now", [P, SLOTS, 3 * TPG], I32)

        big = sb("big", [P, EP])
        xs = sb("xs", [P, SLOTS, GE])
        xd = sb("xd", [P, SLOTS, GE])
        flags = sb("flags", [P, SLOTS, GE], U8)
        xn = sb("xn", [P, 2, 2 * GE])
        hs = sb("hs", [P, 2, GE])
        hd = sb("hd", [P, 2, GE])
        m_a = sb("m_a", [P, 2, GE])
        run = sb("run", [P, 2, GE])
        y_out = sb("y_out", [P, SLOTS, GE])
        ea = sb("ea", [P, SLOTS, TPG * DE])
        eaT = sb("eaT", [DE + 1, 2, GE])
        l_row = sb("l_row", [1, SLOTS, GE])
        logits = sb("logits", [HALF, 2, 2, P])
        weights = sb("weights", [P, TILES])
        sm = sb("sm", [P, 4])
        mrow = sb("mrow", [1, 2])
        bst = sb("bst", [P, 2, 2 * TPG, 6])
        mv = sb("mv", [P, SLOTS, 2 * TPG, 2])
        var = sb("var", [P, 2, 2 * TPG])
        half_bits = sb("half_bits", [P, 2, 2 * TPG], I32)
        newton = sb("newton", [P, 2, 2 * TPG])
        rstd = sb("rstd", [P, SLOTS, 2 * TPG])

        bank = [ctx.enter_context(nc.psum_tensor(f"bank{i}", [P, 512], F32)) for i in range(8)]

        s_fill = sem("s_fill")
        s_index = sem("s_index")
        s_weights = sem("s_weights")
        s_zeroed = sem("s_zeroed")
        s_ident0 = sem("s_ident0")
        s_ident = sem("s_ident")
        s_ones = sem("s_ones")
        s_dve = sem("s_dve")
        s_link = sem("s_link")
        s_same = sem("s_same")
        s_rows = sem("s_rows")
        s_mirrored = sem("s_mirrored")
        s_mirror = sem("s_mirror")
        s_idx_rows = sem("s_idx_rows")
        s_idxT = sem("s_idxT")
        s_idx = sem("s_idx")
        s_flags_dram = sem("s_flags_dram")
        s_wdiff = sem("s_wdiff")
        s_wT = sem("s_wT")
        s_wT_in = sem("s_wT_in")
        s_u = sem("s_u")
        s_u_in = sem("s_u_in")
        s_eaT_ones = sem("s_eaT_ones")
        s_copy = sem("s_copy")
        s_taken = sem("s_taken")
        s_issue = sem("s_issue")
        a_flags = ring("a_flags")
        a_gathered = ring("a_gathered")
        a_copied = sem("a_copied")
        a_normed = sem("a_normed")
        a_turned = sem("a_turned")
        a_relu = sem("a_relu")
        a_msg = sem("a_msg")
        a_biased = sem("a_biased")
        a_max = sem("a_max")
        a_back = sem("a_back")
        a_y = sem("a_y")
        s_spilled = sem("s_spilled")
        s_staged = sem("s_staged")
        s_scattered = ring("s_scattered")
        s_flags = ring("s_flags")
        s_ea = ring("s_ea")
        s_ea_tail = sem("s_ea_tail")
        s_normed = sem("s_normed")
        s_turned = sem("s_turned")
        s_eaT = sem("s_eaT")
        s_hd = sem("s_hd")
        s_first = sem("s_first")
        s_part = sem("s_part")
        s_part_out = ring("s_part_out")
        s_run0 = sem("s_run0")
        b_gathered = ring("b_gathered")
        b_part = ring("b_part")
        b_normed = sem("b_normed")
        b_turned = sem("b_turned")
        b_hs = sem("b_hs")
        b_lout = ring("b_lout")
        b_first = sem("b_first")
        b_sum = sem("b_sum")
        b_logits = sem("b_logits")
        b_g1 = sem("b_g1")
        b_second = sem("b_second")
        b_g2 = sem("b_g2")
        b_third = sem("b_third")
        b_msg = sem("b_msg")
        s_logits0 = sem("s_logits0")
        s_logits_in = sem("s_logits_in")
        s_logits = sem("s_logits")
        s_ladd = sem("s_ladd")
        s_max = sem("s_max")
        s_maxT = sem("s_maxT")
        s_max1 = sem("s_max1")
        s_maxb = sem("s_maxb")
        s_negmax = sem("s_negmax")
        s_exps = sem("s_exps")
        s_sum = sem("s_sum")
        s_inv = sem("s_inv")
        s_turned_exps = sem("s_turned_exps")
        s_exps_in = sem("s_exps_in")
        c_wide = sem("c_wide")
        c_flags = ring("c_flags")
        c_y = ring("c_y")
        c_alpha = sem("c_alpha")
        c_wm = sem("c_wm")
        c_sum = sem("c_sum")
        c_back = sem("c_back")
        c_out = sem("c_out")
        c_scattered = ring("c_scattered")

        def flat(a):
            return a.rearrange("(o n) -> o n", o=1)

        def column(a):
            return a.rearrange("(n o) -> n o", o=1)

        def tile(buf, u, j, width=P):
            return buf[:, u, j * width:(j + 1) * width]

        def segment(n):
            return big[:, bass.ds(n * GE, GE)]

        def whole(dram, n):
            return dram[bass.ds(n, 1), :, :].rearrange("g p n -> p (g n)")

        block = ctx.enter_context(nc.Block())
        N_W = 19
        PIECE = P * (N // (G * P))
        assert (N - G * PIECE) % 8 == 0
        A_GATHERS = 2 * TPG * 16
        GATHERS = TPG * 16

        @block.sync
        def _(sp):
            sp.wait_ge(s_fill, 3)
            for row, a, shift in ((dst_row, dst, 0), (next_row, dst, 1), (src_row, src, 0)):
                mid, end = HALF * P, (TILES - 1) * P
                sp.dma_start(row[:, 0, :], a[shift:mid + shift].rearrange("(t p) -> t p", p=P)
                             ).then_inc(s_index, 16)
                sp.dma_start(row[0:HALF - 1, 1, :], a[mid + shift:end + shift].rearrange("(t p) -> t p", p=P)
                             ).then_inc(s_index, 16)
                sp.dma_start(row[HALF - 1:HALF, 1, 0:TAIL - shift], flat(a[end + shift:E])).then_inc(s_index, 16)
            sp.wait_ge(s_same, 1)
            sp.dma_start(same_dram[:, 0:1], zero_u8[:, :]).then_inc(s_flags_dram, 16)
            for h in range(2):
                sp.dma_start(same_dram[0, 1 + h * HALF * P:1 + (h + 1) * HALF * P].rearrange("(t p) -> t p", p=P),
                             same_u8[:, h, :]).then_inc(s_flags_dram, 16)
            sp.wait_ge(s_mirror, 1)
            for h in range(2):
                sp.dma_start(mirror_dram[0, h * HALF * P:(h + 1) * HALF * P].rearrange("(t p) -> t p", p=P),
                             mirror_u8[:, h, :]).then_inc(s_flags_dram, 16)
            sp.wait_ge(s_flags_dram, 16 * 5)

            def copy_x(first, rows, b):
                sp.dma_start(out[bass.ds(first, rows), :].rearrange("(a b) c -> a (b c)", b=b),
                             x[bass.ds(first, rows), :].rearrange("(a b) c -> a (b c)", b=b)).then_inc(s_copy, 16)

            def flags_a(g):
                over(sp, a_max, ago(g, SLOTS))
                sp.dma_start(flags[:, g[1], :], same_dram[:, bass.ds(number(g) * GE, GE)].broadcast_to([P, GE])
                             ).then_inc(a_flags[g[1]], 16)
                copy_x(number(g) * PIECE, PIECE, PIECE // P)

            def spill(g):
                over(sp, a_y, g)
                sp.dma_start(whole(y_dram, number(g)), segment(number(g))).then_inc(s_spilled, 16)

            copy_x(G * PIECE, N - G * PIECE, 8)
            pipeline(sp, G, [(0, flags_a), (8, spill)])

            full = TPG - 1
            sp.wait_ge(s_fill, 4)
            sp.dma_start(ea[0:TAIL, 0, full * DE:TPG * DE], edge_attr[E - TAIL:E, :]).then_inc(s_ea_tail, 16)

            def inputs_s(g):
                k, u = g
                over(sp, s_hd, ago(g, SLOTS))
                sp.dma_start(flags[:, u, :], mirror_dram[:, bass.ds(number(g) * GE, GE)].broadcast_to([P, GE])
                             ).then_inc(s_flags[u], 16)
                over(sp, s_turned, ago(g, SLOTS))
                n = mirrored(g)
                tiles = full if isinstance(n, int) and n == LAST else TPG
                sp.dma_start(ea[:, u, 0:tiles * DE].rearrange("p (j d) -> p j d", d=DE),
                             edge_attr[bass.ds(n * GE, tiles * P), :].rearrange("(j p) d -> p j d", p=P)
                             ).then_inc(s_ea[u], 16)

            def part_out(g):
                k, u = g
                over(sp, s_part, g)
                sp.dma_start(whole(part_dram, mirrored(g)), xd[:, u, :]).then_inc(s_part_out[u], 16)
                sp.dma_start(logit_dst_dram[:, bass.ds(mirrored(g) * GE, GE)], l_row[:, u, :]
                             ).then_inc(s_part_out[u], 16)

            all_over(sp, a_max)
            pipeline(sp, G, [(0, inputs_s), (7, part_out)])

            all_over(sp, s_part_out, 32)
            sp.wait_ge(s_logits0, 1)

            def logits_in(q, dram, done):
                mid, end = HALF * P, (TILES - 1) * P
                sp.dma_start(logits[:, q, 0, :], dram[0, 0:mid].rearrange("(t p) -> t p", p=P)).then_inc(done, 16)
                sp.dma_start(logits[0:HALF - 1, q, 1, :], dram[0, mid:end].rearrange("(t p) -> t p", p=P)
                             ).then_inc(done, 16)
                sp.dma_start(logits[HALF - 1:HALF, q, 1, 0:TAIL], dram[:, end:E]).then_inc(done, 16)

            logits_in(0, logit_dst_dram, s_logits_in)

            def part_in(g):
                over(sp, b_sum, ago(g, SLOTS))
                sp.dma_start(xd[:, g[1], :], whole(part_dram, number(g))).then_inc(b_part[g[1]], 16)

            def logits_out(g):
                over(sp, b_logits, g)
                sp.dma_start(logit_src_dram[:, bass.ds(number(g) * GE, GE)], l_row[:, g[1], :]
                             ).then_inc(b_lout[g[1]], 16)

            pipeline(sp, G, [(0, part_in), (6, logits_out)])
            all_over(sp, b_lout, 16)
            logits_in(1, logit_src_dram, s_logits_in)

            sp.wait_ge(s_spilled, 16 * G)
            all_over(sp, b_sum)

            def flags_c(g):
                over(sp, c_sum, ago(g, SLOTS))
                sp.dma_start(flags[:, g[1], :], same_dram[:, bass.ds(number(g) * GE, GE)].broadcast_to([P, GE])
                             ).then_inc(c_flags[g[1]], 16)

            def rows_y_c(g):
                over(sp, c_out, ago(g, SLOTS))
                sp.dma_start(xd[:, g[1], :], whole(y_dram, number(g))).then_inc(c_y[g[1]], 16)

            pipeline(sp, G, [(0, flags_c), (0, rows_y_c)])

        @block.gpsimd
        def _(pool):
            taken = Steps(pool, s_taken)
            last_row = pool.to_reg(N - 1)
            pool.memset(dst_row[:, :, :], N).then_inc(s_fill, 1)
            pool.memset(next_row[:, :, :], N).then_inc(s_fill, 1)
            pool.memset(src_row[:, :, :], 0).then_inc(s_fill, 1)
            pool.memset(ident[:, :], 0.0)
            pool.memset(flip[:, :], 0.0).then_inc(s_ident0, 1)
            pool.wait_ge(s_ident0, 1)
            pool.affine_select(out=ident[:, :], in_=ident[:, :], compare_op=ALU.not_equal, fill=1.0, base=0,
                               pattern=[[-1, P]], channel_multiplier=1)
            pool.affine_select(out=flip[:, :], in_=flip[:, :], compare_op=ALU.not_equal, fill=1.0,
                               base=-(HALF - 1), pattern=[[1, HALF]], channel_multiplier=1).then_inc(s_ident, 1)
            pool.memset(weT[:, :], 0.0)
            pool.memset(bnode_last[:, :], 0.0).then_inc(s_zeroed, 1)
            pool.memset(ea[:, 0, :], 0.0).then_inc(s_fill, 1)
            pool.memset(logits[:, :, :, :], LOWEST / 4).then_inc(s_logits0, 1)

            def take(done, each):
                def stage(g):
                    if g[1] % 2 == 0:
                        over(pool, done, ago(g, SLOTS), each)
                        over(pool, done, ago(g, SLOTS - 1), each)
                        taken.inc(pool.tensor_copy(idx_now[:, g[1]:g[1] + 2, :], idx[:, bass.ds(number(g), 2), :]))
                return stage

            def issue(g):
                pool.sem_inc(s_issue, 1)

            def at(u, table, j):
                c = table * TPG + j
                return bass.IndirectOffsetOnAxis(ap=idx_now[:, u, c:c + 1], axis=0)

            def gather(u, buf, table, rows, done):
                for j in range(TPG):
                    pool.indirect_dma_start(tile(buf, u, j), None, rows, at(u, table, j),
                                            bounds_check=last_row, oob_is_err=False).then_inc(done[u], 16)

            def scatter(u, done):
                for j in range(TPG):
                    pool.indirect_dma_start(out, at(u, 2, j), tile(y_out, u, j), None,
                                            bounds_check=last_row, oob_is_err=False).then_inc(done[u], 16)

            pool.wait_ge(s_idx, 1)

            def gather_a(g):
                over(pool, a_normed, ago(g, SLOTS))
                over(pool, a_copied, ago(g, SLOTS))
                taken.wait()
                issue(g)
                gather(g[1], xs, 0, x, a_gathered)
                gather(g[1], xd, 1, x, a_gathered)

            pipeline(pool, G, [(0, take(a_gathered, A_GATHERS)), (0, gather_a)], taken, SLOTS // 2)
            all_over(pool, a_gathered, A_GATHERS)

            pool.wait_ge(s_copy, 16 * (G + 1))

            def scatter_s(g):
                over(pool, s_staged, g)
                taken.wait()
                issue(g)
                scatter(g[1], s_scattered)

            pipeline(pool, G, [(0, take(s_scattered, GATHERS)), (0, scatter_s)], taken, SLOTS // 2)

            all_over(pool, s_scattered, GATHERS)
            all_over(pool, a_normed)

            def gather_b(g):
                over(pool, b_normed, ago(g, SLOTS))
                taken.wait()
                issue(g)
                gather(g[1], xs, 0, out, b_gathered)

            pipeline(pool, G, [(0, take(b_gathered, GATHERS)), (0, gather_b)], taken, SLOTS // 2)
            all_over(pool, b_gathered, GATHERS)

            def scatter_c(g):
                over(pool, c_out, g)
                taken.wait()
                issue(g)
                scatter(g[1], c_scattered)

            pipeline(pool, G, [(0, take(c_scattered, GATHERS)), (0, scatter_c)], taken, SLOTS // 2)
            all_over(pool, c_scattered, GATHERS)

        @block.vector
        def _(dve):
            st = Steps(dve, s_dve)
            dve.memset(zero_u8[:, :], 0)
            dve.memset(one_last[:, :], 0.0)
            dve.memset(eaT[DE:DE + 1, :, :], 1.0).then_inc(s_eaT_ones, 1)
            dve.memset(ones[:, :], 1.0).then_inc(s_ones, 1)
            dve.memset(run[:, 1, GE - 1:GE], 0.0)
            dve.memset(hd[:, 1, 0:1], 0.0).then_inc(s_run0, 1)

            dve.wait_ge(s_index, 16 * 9)
            st.inc(dve.tensor_tensor(same_row[:, :, :], dst_row[:, :, :], next_row[:, :, :], ALU.is_equal))
            dve.tensor_copy(idx_row[:, 0, :, :], src_row[:, :, :])
            dve.tensor_scalar(idx_row[:, 1, :, :], dst_row[:, :, :], float(N - 1), None, ALU.min)
            st.wait()
            dve.scalar_tensor_tensor(out=idx_row[:, 2, :, :], in0=same_row[:, :, :], scalar=float(SKIP),
                                     in1=dst_row[:, :, :], op0=ALU.mult, op1=ALU.add).then_inc(s_idx_rows, 1)
            dve.tensor_copy(same_u8[:, :, :], same_row[:, :, :]).then_inc(s_same, 1)
            for h in range(2):
                ins = dve.tensor_copy(mirror_row[:, h, :], same_row[:, h, ::-1])
            ins.then_inc(s_mirrored, 1)
            dve.memset(idx[:, G, :], 0)
            dve.wait_ge(s_idxT, 1)
            for table in range(3):
                dve.tensor_copy(idx[:, 0:G, table * TPG:(table + 1) * TPG],
                                bank[table][:, 0:TILES].rearrange("p (g j) -> p g j", j=TPG))
            dve.tensor_scalar(is_last[:, :, :], bank[2][:, 0:TILES].rearrange("p (g j) -> p g j", j=TPG),
                              float(SKIP), None, ALU.is_lt).then_inc(s_idx, 1)
            for h in range(2):
                ins = dve.tensor_copy(mirror_u8[:, 1 - h, :], bank[3][0:HALF, h * P:(h + 1) * P])
            ins.then_inc(s_mirror, 1)

            dve.wait_ge(s_weights, 16 * N_W)
            dve.wait_ge(s_eaT_ones, 1)
            dve.memset(one_last[:, DE:DE + 1], 1.0)
            dve.tensor_tensor(w0_dst[:, :], w0_dst[:, :], w0_src[:, :], ALU.subtract).then_inc(s_wdiff, 1)
            dve.wait_ge(s_wT, 1)
            dve.tensor_copy(wnT[:, :], bank[4][:, 0:P])
            dve.tensor_copy(weT[:, 0:DE], bank[5][:, 0:DE]).then_inc(s_wT_in, 1)
            dve.wait_ge(s_u, 1)
            dve.tensor_copy(u_src[:, :], bank[6][:, 0:1])
            dve.tensor_copy(u_dst[:, :], bank[6][:, 1:2])
            dve.tensor_copy(u_edge[:, :], bank[7][0:DE + 1, 0:1]).then_inc(s_u_in, 1)

            LN_LINKS = 13

            def stats(g, tiles):
                for j, t in enumerate(tiles):
                    ins = dve.bn_stats(bst[:, g[1] % 2, j, :], t)
                st.inc(ins)

            def norm_links(slots, m, mask_of=None):
                n0, q = st.n, len(slots)
                st.wait()
                dve.sem_inc(s_link, 1)
                for u in slots:
                    for j in range(m):
                        ins = dve.bn_aggr(mv[:, u, j, :], bst[:, u % 2, j, :])
                st.inc(ins)
                yield
                u0 = slots[0]
                v, y, t, h = var[:, 0:q, 0:m], rstd[:, u0:u0 + q, 0:m], newton[:, 0:q, 0:m], half_bits[:, 0:q, 0:m]
                st.wait()
                st.inc(dve.tensor_scalar(v, mv[:, u0:u0 + q, 0:m, 1], EPS, None, ALU.add))
                yield
                st.wait()
                st.inc(dve.tensor_scalar(h, v.bitcast(I32), 1, None, ALU.logical_shift_right))
                yield
                st.wait()
                st.inc(dve.tensor_scalar(y.bitcast(I32), h, -1.0, float(RSQRT_SEED), ALU.mult, ALU.add))
                yield
                for step in range(3):
                    st.wait()
                    st.inc(dve.scalar_tensor_tensor(out=t, in0=y, scalar=-0.5, in1=y, op0=ALU.mult,
                                                    op1=ALU.mult))
                    yield
                    st.wait()
                    if step == 2 and mask_of is not None:
                        for u in slots:
                            dve.tensor_tensor(rstd[:, u, 0:m], rstd[:, u, 0:m], mask_of(u), ALU.mult)
                    st.inc(dve.tensor_tensor(t, t, v, ALU.mult))
                    yield
                    st.wait()
                    st.inc(dve.scalar_tensor_tensor(out=y, in0=t, scalar=1.5, in1=y, op0=ALU.add, op1=ALU.mult))
                    yield
                assert st.n - n0 == LN_LINKS, st.n - n0

            LN_STEPS = SLOTS + SLOTS // 2 * LN_LINKS

            def norms(g, live, tiles_of, m, mask_of=None):
                if live(0):
                    stats(g, tiles_of(g))
                if g[1] % 2 and live(1):
                    slots = [g[1] - 1, g[1]] if live(0) else [g[1] - 1]
                    return norm_links(slots, m, mask_of and (lambda u: mask_of(g if u == g[1] else ago(g, 1))))
                return iter(())

            def links_done(g, live):
                if not (g[1] % 2 and live(1)):
                    st.wait(1 if live(0) else 0)

            def apply(g, tiles, j, done):
                u = g[1]
                ins = dve.tensor_scalar(tile(xn, u % 2, j), tiles[j], mv[:, u, j, 0:1], rstd[:, u, j:j + 1],
                                        ALU.subtract, ALU.mult)
                if j == len(tiles) - 1:
                    ins.then_inc(done, 1)

            def tiles_a(g):
                return [tile(buf, g[1], j) for buf in (xs, xd) for j in range(TPG)]

            def max_a(g):
                u, d = g[1], g[1] % 2
                over(dve, a_biased, g)
                over(dve, a_flags, g, 16)
                over(dve, a_back, ago(g, 2))
                over(dve, a_max, ago(g, 1))
                dve.tensor_tensor_scan(run[:, d, :], flags[:, u, :], m_a[:, d, :], run[:, 1 - d, GE - 1:GE],
                                       ALU.mult, ALU.max).then_inc(a_max, 1)

            def add_y(g):
                over(dve, a_back, g)
                over(dve, a_copied, g)
                dve.tensor_tensor(segment(number(g)), bank[6 + g[1] % 2][:, :], segment(number(g)), ALU.add
                                  ).then_inc(a_y, 1)

            def step_a(g, live):
                if live(0):
                    over(dve, a_gathered, g, A_GATHERS)
                chain = norms(g, live, tiles_a, 2 * TPG)
                next(chain, None)
                if live(2):
                    links_done(g, live)
                    over(dve, a_turned, ago(g, 4))
                    for j in range(2 * TPG):
                        apply(ago(g, 2), tiles_a(ago(g, 2)), j, a_normed)
                        next(chain, None)
                if live(4):
                    max_a(ago(g, 4))
                next(chain, None)
                if live(5):
                    add_y(ago(g, 5))
                for _ in chain:
                    pass

            dve.wait_ge(s_run0, 1)
            in_steps(dve, G, 5, step_a, st, LN_STEPS)

            def tiles_s(g):
                return [big[:, bass.ds(mirrored(g) * GE + j * P, P)] for j in range(TPG)]

            def spread_s(g):
                u, d = g[1], g[1] % 2
                over(dve, s_turned, g)
                over(dve, s_flags, g, 16)
                over(dve, s_first, ago(g, 2))
                over(dve, s_hd, ago(g, 1))
                dve.tensor_tensor_scan(hd[:, d, ::-1], flags[:, u, :], bank[d][:, ::-1],
                                       hd[:, 1 - d, 0:1], ALU.mult, ALU.max).then_inc(s_hd, 1)

            def step_s(g, live):
                chain = norms(g, live, tiles_s, TPG, lambda g: is_last[:, bass.ds(mirrored(g), 1), :]
                              .rearrange("p g j -> p (g j)"))
                next(chain, None)
                if live(2):
                    links_done(g, live)
                    over(dve, s_turned, ago(g, 4))
                    for j in range(TPG):
                        apply(ago(g, 2), tiles_s(ago(g, 2)), j, s_normed)
                        next(chain, None)
                if live(3):
                    spread_s(ago(g, 3))
                for _ in chain:
                    pass

            all_over(dve, a_y)
            all_over(dve, a_msg)
            dve.memset(hd[:, 1, 0:1], 0.0).then_inc(s_run0, 1)
            dve.wait_ge(s_run0, 2)
            in_steps(dve, G, 3, step_s, st, LN_STEPS)

            def tiles_b(g):
                return [tile(xs, g[1], j) for j in range(TPG)]

            def sum_b(g):
                u, d = g[1], g[1] % 2
                over(dve, b_first, g)
                over(dve, b_part, g, 16)
                over(dve, b_g1, ago(g, 2))
                dve.tensor_tensor(hd[:, d, :], bank[2 + d][:, :], xd[:, u, :], ALU.add).then_inc(b_sum, 1)

            def step_b(g, live):
                if live(0):
                    over(dve, b_gathered, g, GATHERS)
                chain = norms(g, live, tiles_b, TPG)
                next(chain, None)
                if live(2):
                    links_done(g, live)
                    over(dve, b_turned, ago(g, 4))
                    for j in range(TPG):
                        apply(ago(g, 2), tiles_b(ago(g, 2)), j, b_normed)
                        next(chain, None)
                if live(4):
                    sum_b(ago(g, 4))
                for _ in chain:
                    pass

            all_over(dve, s_first)
            in_steps(dve, G, 4, step_b, st, LN_STEPS)

            dve.wait_ge(s_logits_in, 16 * 6)
            dve.tensor_tensor(logits[:, 0, :, :], logits[:, 0, :, :], logits[:, 1, :, :], ALU.add
                              ).then_inc(s_ladd, 1)
            dve.wait_ge(s_ladd, 1)
            dve.tensor_reduce(sm[0:HALF, 0:1], logits[:, 0, :, :].rearrange("t h p -> t (h p)"), AX_X, ALU.max
                              ).then_inc(s_max, 1)
            dve.wait_ge(s_maxT, 1)
            dve.tensor_reduce(mrow[:, 0:1], bank[0][0:1, 0:HALF], AX_X, ALU.max).then_inc(s_max1, 1)
            dve.wait_ge(s_maxb, 1)
            dve.tensor_scalar(sm[:, 1:2], bank[1][:, 0:1], -1.0, None, ALU.mult).then_inc(s_negmax, 1)
            dve.wait_ge(s_sum, 1)
            dve.reciprocal(sm[:, 3:4], bank[2][:, 0:1]).then_inc(s_inv, 1)
            dve.wait_ge(s_turned_exps, 1)
            dve.tensor_copy(weights[:, :], bank[3][:, 0:TILES]).then_inc(s_exps_in, 1)
            all_over(dve, b_third)
            dve.memset(run[:, 1, GE - 1:GE], 0.0).then_inc(s_run0, 1)
            dve.wait_ge(s_run0, 3)

            def weigh(g):
                u, d = g[1], g[1] % 2
                over(dve, c_alpha, g)
                over(dve, c_sum, ago(g, 2))
                dve.tensor_tensor(hd[:, d, :], segment(number(g)), bank[d][:, :], ALU.mult).then_inc(c_wm, 1)

            def sum_c(g):
                u, d = g[1], g[1] % 2
                over(dve, c_wm, g)
                over(dve, c_flags, g, 16)
                over(dve, c_back, ago(g, 2))
                over(dve, c_sum, ago(g, 1))
                dve.tensor_tensor_scan(run[:, d, :], flags[:, u, :], hd[:, d, :], run[:, 1 - d, GE - 1:GE],
                                       ALU.mult, ALU.add).then_inc(c_sum, 1)

            def add_out(g):
                u, d = g[1], g[1] % 2
                over(dve, c_back, g)
                over(dve, c_y, g, 16)
                over(dve, c_scattered, ago(g, SLOTS), GATHERS)
                dve.tensor_tensor(y_out[:, u, :], bank[6 + d][:, :], xd[:, u, :], ALU.add).then_inc(c_out, 1)

            all_over(dve, b_msg)
            pipeline(dve, G, [(1, weigh), (2, sum_c), (4, add_out)])

        @block.tensor
        def _(pe):
            def turn(dest, source, rows=P):
                for j in range(TPG):
                    ins = pe.transpose(dest[0:rows, j * P:(j + 1) * P], source(j), ident[:, :])
                return ins

            pe.wait_ge(s_ident, 1)
            pe.wait_ge(s_idx_rows, 1)
            for table in range(3):
                for h in range(2):
                    ins = pe.transpose(bank[table][:, h * HALF:(h + 1) * HALF], idx_row[:, table, h, :],
                                       ident[0:HALF, 0:HALF])
            pe.wait_ge(s_mirrored, 1)
            for h in range(2):
                ins = pe.matmul(bank[3][0:HALF, h * P:(h + 1) * P], flip[:, :], mirror_row[:, h, :],
                                start=True, stop=True)
            ins.then_inc(s_idxT, 1)
            pe.wait_ge(s_weights, 16 * N_W)
            pe.transpose(bank[4][:, 0:P], wn[:, :], ident[:, :])
            pe.transpose(bank[5][:, 0:DE], we[:, :], ident[0:DE, 0:DE]).then_inc(s_wT, 1)
            pe.wait_ge(s_wdiff, 1)
            pe.wait_ge(s_wT_in, 1)
            pe.matmul(bank[6][:, 0:1], wnT[:, :], watt[:, 0:1], start=True, stop=True)
            pe.matmul(bank[6][:, 1:2], wnT[:, :], watt[:, 1:2], start=True, stop=True)
            const = bank[7][0:DE + 1, 0:1]
            pe.matmul(const, weT[:, :], watt[:, 2:3], start=True, stop=False)
            pe.matmul(const, bnode_last[:, :], watt[:, 0:1], start=False, stop=False)
            pe.matmul(const, bnode_last[:, :], watt[:, 1:2], start=False, stop=False)
            pe.matmul(const, one_last[:, :], batt[:, :], start=False, stop=True).then_inc(s_u, 1)
            pe.wait_ge(s_u_in, 1)

            def turn_a(g):
                d = g[1] % 2
                over(pe, a_normed, g)
                over(pe, a_relu, ago(g, 2))
                turn(bank[d], lambda j: tile(xn, d, j))
                turn(bank[2 + d], lambda j: tile(xn, d, TPG + j)).then_inc(a_turned, 1)

            def messages_a(g):
                d = g[1] % 2
                over(pe, a_relu, g)
                over(pe, a_biased, ago(g, 2))
                pe.matmul(bank[4 + d][:, :], w0_src[:, :], hs[:, d, :], start=True, stop=False)
                pe.matmul(bank[4 + d][:, :], w0_dst[:, :], hd[:, d, :], start=False, stop=True
                          ).then_inc(a_msg, 1)

            def back_a(g):
                d = g[1] % 2
                over(pe, a_max, g)
                over(pe, a_y, ago(g, 2))
                turn(bank[6 + d], lambda j: tile(run, d, j)).then_inc(a_back, 1)

            pipeline(pe, G, [(2, turn_a), (3, messages_a), (4, back_a)])

            def turn_s(g):
                u, d = g[1], g[1] % 2
                over(pe, s_normed, g)
                over(pe, s_ea, g, 16)
                over(pe, s_hd, ago(g, 2))
                over(pe, s_eaT, ago(g, 2))
                turn(bank[d], lambda j: tile(xn, d, j))
                turn(bank[2 + d], lambda j: tile(ea, u, j, DE), DE).then_inc(s_turned, 1)

            def first_s(g):
                u, d = g[1], g[1] % 2
                over(pe, s_hd, g)
                over(pe, s_eaT, g)
                over(pe, s_part, ago(g, 2))
                for dest, w_d, w_e in ((bank[4 + d][:, :], w1_dst, w1_edge),
                                       (bank[6 + d][0:1, :], u_dst, u_edge)):
                    pe.matmul(dest, w_e[:, :], eaT[:, d, :], start=True, stop=False)
                    ins = pe.matmul(dest, w_d[:, :], hd[:, d, :], start=False, stop=True)
                ins.then_inc(s_first, 1)

            all_over(pe, a_y)
            pe.wait_ge(s_ea_tail, 16)
            pipeline(pe, G, [(2, turn_s), (4, first_s)])

            def turn_b(g):
                d = g[1] % 2
                over(pe, b_normed, g)
                over(pe, b_hs, ago(g, 2))
                turn(bank[d], lambda j: tile(xn, d, j)).then_inc(b_turned, 1)

            def first_b(g):
                d = g[1] % 2
                over(pe, b_hs, g)
                over(pe, b_sum, ago(g, 2))
                over(pe, b_logits, ago(g, 2))
                pe.matmul(bank[2 + d][:, :], w1_src[:, :], hs[:, d, :], start=True, stop=True)
                pe.matmul(bank[4 + d][0:1, :], u_src[:, :], hs[:, d, :], start=True, stop=True
                          ).then_inc(b_first, 1)

            def second_b(g):
                over(pe, b_g1, g)
                over(pe, b_g2, ago(g, 1))
                pe.matmul(bank[6][:, :], w2[:, :], m_a[:, g[1] % 2, :], start=True, stop=True
                          ).then_inc(b_second, 1)

            def third_b(g):
                over(pe, b_g2, g)
                over(pe, b_msg, ago(g, 1))
                pe.matmul(bank[7][:, :], w3[:, :], run[:, g[1] % 2, :], start=True, stop=True
                          ).then_inc(b_third, 1)

            all_over(pe, s_part)
            def step_b(g, live):
                for lag, stage in ((2, turn_b), (3, first_b), (6, second_b), (7, third_b)):
                    if live(lag):
                        stage(ago(g, lag))
                if live(6) and not live(5):
                    pe.wait_ge(s_max, 1)
                    all_over(pe, b_hs)
                    pe.transpose(bank[0][0:1, 0:HALF], sm[0:HALF, 0:1], ident[0:HALF, 0:HALF]).then_inc(s_maxT, 1)
                if live(7) and not live(6):
                    pe.wait_ge(s_max1, 1)
                    pe.matmul(bank[1][:, 0:1], ones[0:1, :], mrow[:, 0:1], start=True, stop=True
                              ).then_inc(s_maxb, 1)

            in_steps(pe, G, 7, step_b)

            pe.wait_ge(s_exps, 1)
            all_over(pe, b_sum)
            pe.matmul(bank[2][:, 0:1], ones[0:HALF, :], sm[0:HALF, 2:3], start=True, stop=True).then_inc(s_sum, 1)
            for h in range(2):
                ins = pe.transpose(bank[3][:, h * HALF:(h + 1) * HALF], logits[:, 1, h, :], ident[0:HALF, 0:HALF])
            ins.then_inc(s_turned_exps, 1)

            def spread_c(g):
                d = g[1] % 2
                over(pe, c_wide, g)
                over(pe, c_wm, ago(g, 2))
                turn(bank[d], lambda j: tile(m_a, d, j)).then_inc(c_alpha, 1)

            def back_c(g):
                d = g[1] % 2
                over(pe, c_sum, g)
                over(pe, c_out, ago(g, 2))
                turn(bank[6 + d], lambda j: tile(run, d, j)).then_inc(c_back, 1)

            all_over(pe, b_msg)
            pipeline(pe, G, [(0, spread_c), (2, back_c)])

        @block.scalar
        def _(act):
            for dest, a in ((w0_dst[:, :], W0[0:C, :]), (w0_src[:, :], W0[C:2 * C, :]),
                            (w1_src[:, :], W_m1[0:C, :]), (w1_dst[:, :], W_m1[C:2 * C, :]),
                            (w1_edge[0:DE, :], W_m1[2 * C:2 * C + DE, :]), (w1_edge[DE:DE + 1, :], flat(b_m1)),
                            (w2[:, :], W_m2), (w3[:, :], W_m3), (wn[:, :], W_node), (we[:, :], W_edge),
                            (col[:, 0:1], column(b0)), (col[:, 1:2], column(b_m2)), (col[:, 2:3], column(b_m3)),
                            (watt[:, 0:1], W_att[0:P, :]), (watt[:, 1:2], W_att[P:2 * P, :]),
                            (watt[:, 2:3], W_att[2 * P:3 * P, :]), (batt[:, :], flat(b_att))):
                act.dma_start(dest, a).then_inc(s_weights, 16)
            act.wait_ge(s_zeroed, 1)
            act.dma_start(bnode_last[:, DE:DE + 1], column(b_node)).then_inc(s_weights, 16)
            act.dma_start(weT[:, DE:DE + 1], column(b_edge)).then_inc(s_weights, 16)

            def copy_a(g):
                over(act, a_gathered, g, A_GATHERS)
                act.activation(segment(number(g)), xd[:, g[1], :], ACT.Copy).then_inc(a_copied, 1)

            def relu_a(g):
                d = g[1] % 2
                over(act, a_turned, g)
                over(act, a_msg, ago(g, 2))
                act.activation(hs[:, d, :], bank[d][:, :], ACT.Relu)
                act.activation(hd[:, d, :], bank[2 + d][:, :], ACT.Relu).then_inc(a_relu, 1)

            def bias_a(g):
                d = g[1] % 2
                over(act, a_msg, g)
                over(act, a_max, ago(g, 2))
                act.activation(m_a[:, d, :], bank[4 + d][:, :], ACT.Identity, bias=col[:, 0:1]
                               ).then_inc(a_biased, 1)

            act.wait_ge(s_weights, 16 * N_W)
            act.wait_ge(s_run0, 1)
            def stage_s(g):
                over(act, a_y, g)
                over(act, s_scattered, ago(g, SLOTS), GATHERS)
                act.activation(y_out[:, g[1], :], segment(number(g)), ACT.Copy).then_inc(s_staged, 1)

            def first_stages():
                for u in range(SLOTS):
                    stage_s((0, u))

            pipeline(act, G, [(0, copy_a), (2, relu_a), (3, bias_a)], before_drain=first_stages)

            def edge_s(g):
                d = g[1] % 2
                over(act, s_turned, g)
                over(act, s_first, ago(g, 2))
                act.activation(eaT[0:DE, d, :], bank[2 + d][0:DE, :], ACT.Copy).then_inc(s_eaT, 1)

            def part_s(g):
                u, d = g[1], g[1] % 2
                over(act, s_first, g)
                over(act, s_part_out, ago(g, SLOTS), 32)
                act.activation(xd[:, u, :], bank[4 + d][:, :], ACT.Copy)
                act.activation(l_row[:, u, :], bank[6 + d][0:1, :], ACT.Copy).then_inc(s_part, 1)

            pipeline(act, G, [(-SLOTS, stage_s), (3, edge_s), (5, part_s)])

            def relu_b(g):
                d = g[1] % 2
                over(act, b_turned, g)
                over(act, b_first, ago(g, 2))
                act.activation(hs[:, d, :], bank[d][:, :], ACT.Relu).then_inc(b_hs, 1)

            def logits_b(g):
                u, d = g[1], g[1] % 2
                over(act, b_first, g)
                over(act, b_lout, ago(g, SLOTS), 16)
                act.activation(l_row[:, u, :], bank[4 + d][0:1, :], ACT.Copy).then_inc(b_logits, 1)

            def gelu1_b(g):
                d = g[1] % 2
                over(act, b_sum, g)
                over(act, b_second, ago(g, 2))
                act.activation(m_a[:, d, :], hd[:, d, :], ACT.Gelu_apprx_tanh).then_inc(b_g1, 1)

            def gelu2_b(g):
                d = g[1] % 2
                over(act, b_second, g)
                over(act, b_third, ago(g, 2))
                act.activation(run[:, d, :], bank[6][:, :], ACT.Gelu_apprx_tanh, bias=col[:, 1:2]
                               ).then_inc(b_g2, 1)

            def exponentials():
                act.wait_ge(s_negmax, 1)
                act.activation(logits[:, 1, :, :].rearrange("t h p -> t (h p)"),
                               logits[:, 0, :, :].rearrange("t h p -> t (h p)"), ACT.Exp,
                               bias=sm[0:HALF, 1:2], accum_out=sm[0:HALF, 2:3]).then_inc(s_exps, 1)

            def message_b(g):
                if isinstance(g[0], int) and number(g) == LAST:
                    exponentials()
                over(act, b_third, g)
                act.activation(segment(number(g)), bank[7][:, :], ACT.Identity, bias=col[:, 2:3]
                               ).then_inc(b_msg, 1)

            all_over(act, s_staged)
            all_over(act, s_normed)
            all_over(act, s_part_out, 32)
            act.wait_ge(s_spilled, 16 * G)
            pipeline(act, G, [(2, relu_b), (4, logits_b), (5, gelu1_b), (6, gelu2_b), (7, message_b)])

            def wide_c(g):
                d = g[1] % 2
                over(act, c_alpha, ago(g, 2))
                act.activation(m_a[:, d, :].rearrange("p (j c) -> p j c", c=P),
                               weights[:, bass.ds(number(g) * TPG, TPG)].rearrange("p (j c) -> p j c", c=1)
                               .broadcast_to([P, TPG, P]), ACT.Identity, scale=sm[:, 3:4]).then_inc(c_wide, 1)

            act.wait_ge(s_inv, 1)
            act.wait_ge(s_exps_in, 1)
            all_over(act, b_second)
            pipeline(act, G, [(0, wide_c)])


_INS = ['x', 'src', 'dst', 'edge_attr_64', 'L0_gnn_W', 'L0_gnn_b', 'L1_gnn_W_node', 'L1_gnn_b_node',
        'L1_gnn_W_edge', 'L1_gnn_b_edge', 'L1_gnn_W_att', 'L1_gnn_b_att', 'L1_gnn_W_m1', 'L1_gnn_b_m1',
        'L1_gnn_W_m2', 'L1_gnn_b_m2', 'L1_gnn_W_m3', 'L1_gnn_b_m3']


def kernel(**inputs):
    import numpy as _np
    import concourse.bacc as _bacc
    from concourse import mybir as _mybir
    from concourse.bass_utils import run_bass_kernel_spmd as _run

    nc = _bacc.Bacc("TRN2", target_bir_lowering=False, num_devices=1)
    arrays, args = {}, []
    for name in _INS:
        a = _np.ascontiguousarray(inputs[name])
        arrays[f"in_{name}_dram"] = a
        args.append(nc.dram_tensor(f"in_{name}_dram", a.shape, _mybir.dt.from_np(a.dtype), kind="ExternalInput").ap())
    shape = tuple(inputs["x"].shape)
    out = nc.dram_tensor("out_0_dram", shape, _mybir.dt.float32, kind="ExternalOutput").ap()
    gnn_kernel(nc, *args, out)
    r = _run(nc, [arrays], core_ids=[0])
    return r.results[0]["out_0_dram"]
```

```python
from contextlib import ExitStack

import concourse.bass as bass
from concourse import mybir

F32 = mybir.dt.float32
I32 = mybir.dt.int32
U8 = mybir.dt.uint8
ALU = mybir.AluOpType
ACT = mybir.ActivationFunctionType
AX_X = mybir.AxisListType.X

P = 128
TPG = 4
GE = TPG * P
SLOTS = 4
EPS = 1e-5
SKIP = 1 << 20
LOWEST = -3.0e38
RSQRT_SEED = 0x5F3759DF


class Steps:

    def __init__(self, eng, sem):
        self.eng, self.sem, self.base, self.n = eng, sem, 0, 0

    def inc(self, ins):
        ins.then_inc(self.sem, 1)
        self.n += 1

    def wait(self, later=0):
        self.eng.wait_ge(self.sem, self.base + (self.n - later))

    def enter(self, i, per_body):
        self.before, self.per_body = self.base + self.n, per_body
        self.base, self.n = self.before + i * per_body, 0

    def leave(self, trips):
        assert self.n == self.per_body, (self.n, self.per_body)
        self.base, self.n = self.before + trips * self.per_body, 0


def ago(g, d):
    k, u = g
    back = -((u - d) // SLOTS)
    return k - back, u - d + SLOTS * back


def over(eng, signal, g, each=1):
    k, u = g
    if isinstance(k, int) and k < 0:
        return
    if isinstance(signal, list):
        eng.wait_ge(signal[u], each * (k + 1))
    else:
        eng.wait_ge(signal, k * SLOTS + (u + 1))


def in_steps(eng, groups, deep, step, steps=None, per_loop=0, ahead=0, before_drain=None):
    first = deep + SLOTS
    first += (groups - ahead - first) % SLOTS
    trips = (groups - ahead - first) // SLOTS

    def peeled(m):
        step((m // SLOTS, m % SLOTS), lambda d: 0 <= m - d < groups)

    for m in range(first):
        peeled(m)
    with eng.Fori(0, trips) as i:
        if steps:
            steps.enter(i, per_loop)
        for m in range(first, first + SLOTS):
            step((i + m // SLOTS, m % SLOTS), lambda d: True)
    if steps:
        steps.leave(trips)
    for m in range(groups - ahead, groups + deep):
        if m == groups - ahead and before_drain:
            before_drain()
        peeled(m)


def pipeline(eng, groups, stages, steps=None, per_loop=0, ahead=0, before_drain=None):
    def step(g, live):
        for lag, stage in stages:
            if live(lag):
                stage(ago(g, lag))

    in_steps(eng, groups, max(lag for lag, _ in stages), step, steps, per_loop,
             max(ahead, -min(lag for lag, _ in stages)), before_drain)


def gnn_kernel(nc, x, src, dst, edge_attr, W0, b0, W_node, b_node, W_edge, b_edge, W_att, b_att,
               W_m1, b_m1, W_m2, b_m2, W_m3, b_m3, out):
    N, C = x.shape
    E, DE = edge_attr.shape
    TILES = -(-E // GE) * TPG
    G = TILES // TPG
    EP = TILES * P
    HALF = TILES // 2
    TAIL = E - (TILES - 1) * P
    LAST = G - 1
    assert C == P and 0 < TAIL <= P and TILES % 2 == 0 and HALF <= P

    def number(g):
        return g[0] * SLOTS + g[1]

    def mirrored(g):
        return (LAST - g[1]) + g[0] * -SLOTS

    with ExitStack() as ctx:
        def sb(name, shape, dt=F32):
            return ctx.enter_context(nc.sbuf_tensor(name, shape, dt))

        def sem(name):
            return ctx.enter_context(nc.semaphore(name))

        def ring(name):
            return [sem(f"{name}{u}") for u in range(SLOTS)]

        def all_over(eng, signal, each=1):
            for n in range(G - SLOTS, G) if isinstance(signal, list) else (LAST,):
                over(eng, signal, (n // SLOTS, n % SLOTS), each)

        src_sorted = nc.dram_tensor("src_sorted", [EP, 1], I32).ap()
        dst_sorted = nc.dram_tensor("dst_sorted", [EP, 1], I32).ap()
        edge_attr_sorted = nc.dram_tensor("edge_attr_sorted", [EP, DE], F32).ap()
        same_dram = nc.dram_tensor("same_dram", [1, EP + 1], U8).ap()
        mirror_dram = nc.dram_tensor("mirror_dram", [1, EP], U8).ap()
        y_dram = nc.dram_tensor("y_dram", [G, P, GE], F32).ap()
        logit_dst_dram = nc.dram_tensor("logit_dst_dram", [1, EP], F32).ap()
        logit_src_dram = nc.dram_tensor("logit_src_dram", [1, EP], F32).ap()
        part_dram = nc.dram_tensor("part_dram", [G, P, GE], F32).ap()

        ident = sb("ident", [P, P])
        flip = sb("flip", [HALF, HALF])
        ones = sb("ones", [P, P])
        w0_dst = sb("w0_dst", [P, P])
        w0_src = sb("w0_src", [P, P])
        w1_src = sb("w1_src", [P, P])
        w1_dst = sb("w1_dst", [P, P])
        w1_edge = sb("w1_edge", [DE + 1, P])
        w2 = sb("w2", [P, P])
        w3 = sb("w3", [P, P])
        wn = sb("wn", [P, P])
        we = sb("we", [DE, P])
        wnT = sb("wnT", [P, P])
        weT = sb("weT", [P, DE + 1])
        bnode_last = sb("bnode_last", [P, DE + 1])
        one_last = sb("one_last", [1, DE + 1])
        col = sb("col", [P, 3])
        watt = sb("watt", [P, 3])
        batt = sb("batt", [1, 1])
        u_src = sb("u_src", [P, 1])
        u_dst = sb("u_dst", [P, 1])
        u_edge = sb("u_edge", [P, DE + 1])

        dst_row = sb("dst_row", [HALF, 2, P], I32)
        next_row = sb("next_row", [HALF, 2, P], I32)
        src_row = sb("src_row", [HALF, 2, P], I32)
        same_row = sb("same_row", [HALF, 2, P])
        mirror_row = sb("mirror_row", [HALF, 2, P])
        same_u8 = sb("same_u8", [HALF, 2, P], U8)
        mirror_u8 = sb("mirror_u8", [HALF, 2, P], U8)
        zero_u8 = sb("zero_u8", [1, 1], U8)
        descents = sb("descents", [HALF, 1])
        unsorted = sb("unsorted", [1, 1], I32)
        lower = sb("lower", [P, P])
        square = sb("square", [P, P])
        below = sb("below", [P, EP // 4], U8)
        own = sb("own", [P, 1])
        counts = sb("counts", [P, 6])
        ranks = sb("ranks", [P, TILES], I32)
        rank_now = sb("rank_now", [P, 1], I32)
        src_now = sb("src_now", [P, 1], I32)
        dst_now = sb("dst_now", [P, 1], I32)
        idx_row = sb("idx_row", [HALF, 3, 2, P])
        idx = sb("idx", [P, G + 1, 3 * TPG], I32)
        is_last = sb("is_last", [P, G, TPG])
        idx_now = sb("idx_now", [P, 2, SLOTS, 3 * TPG], I32)

        big = sb("big", [P, EP])
        xs = sb("xs", [P, SLOTS, GE])
        xd = sb("xd", [P, SLOTS, GE])
        flags = sb("flags", [P, SLOTS, GE], U8)
        xn = sb("xn", [P, 2, 2 * GE])
        hs = sb("hs", [P, 2, GE])
        hd = sb("hd", [P, 2, GE])
        m_a = sb("m_a", [P, 2, GE])
        run = sb("run", [P, 2, GE])
        y_out = sb("y_out", [P, SLOTS, GE])
        ea = sb("ea", [P, SLOTS, TPG * DE])
        product = sb("product", [P, TPG, DE])
        logits_edge = sb("logits_edge", [P, TILES])
        edge_rows = sb("edge_rows", [HALF, 2, P])
        eaT = sb("eaT", [DE + 1, 2, GE])
        l_row = sb("l_row", [1, SLOTS, GE])
        logits = sb("logits", [HALF, 2, 2, P])
        weights = sb("weights", [P, TILES])
        sm = sb("sm", [P, 4])
        mrow = sb("mrow", [1, 2])
        bst = sb("bst", [P, 2, 2 * TPG, 6])
        mv = sb("mv", [P, SLOTS, 2 * TPG, 2])
        var = sb("var", [P, 2, 2 * TPG])
        newton = sb("newton", [P, 2, 2, 2 * TPG])
        rstd = sb("rstd", [P, SLOTS, 2 * TPG])

        bank = [ctx.enter_context(nc.psum_tensor(f"bank{i}", [P, 512], F32)) for i in range(8)]

        s_fill = sem("s_fill")
        s_index = sem("s_index")
        s_index_src = sem("s_index_src")
        s_weights = sem("s_weights")
        s_zeroed = sem("s_zeroed")
        s_ident0 = sem("s_ident0")
        s_ident = sem("s_ident")
        s_ones = sem("s_ones")
        s_dve = sem("s_dve")
        s_link = sem("s_link")
        s_same = sem("s_same")
        a_rows = sem("a_rows")
        s_rows = sem("s_rows")
        b_rows = sem("b_rows")
        c_rows = sem("c_rows")
        s_mirrored = sem("s_mirrored")
        s_mirror = sem("s_mirror")
        s_idx_rows = sem("s_idx_rows")
        s_idxT = sem("s_idxT")
        s_idx = sem("s_idx")
        s_flags_dram = sem("s_flags_dram")
        s_wdiff = sem("s_wdiff")
        s_wT = sem("s_wT")
        s_wT_in = sem("s_wT_in")
        s_u = sem("s_u")
        s_u_in = sem("s_u_in")
        s_eaT_ones = sem("s_eaT_ones")
        s_copy = sem("s_copy")
        s_issue = sem("s_issue")
        s_descents = sem("s_descents")
        s_descents_sum = sem("s_descents_sum")
        s_unsorted = sem("s_unsorted")
        u_dst_in = sem("u_dst_in")
        u_step = sem("u_step")
        u_lower0 = sem("u_lower0")
        u_lower = sem("u_lower")
        u_ranked = sem("u_ranked")
        u_in = sem("u_in")
        u_taken = sem("u_taken")
        u_out = sem("u_out")
        u_index = sem("u_index")
        a_flags = ring("a_flags")
        a_gathered = ring("a_gathered")
        a_ea = ring("a_ea")
        a_product = sem("a_product")
        a_edge = sem("a_edge")
        a_copied = sem("a_copied")
        a_normed = sem("a_normed")
        a_turned = sem("a_turned")
        a_relu = sem("a_relu")
        a_msg = sem("a_msg")
        a_biased = sem("a_biased")
        a_max = sem("a_max")
        a_back = sem("a_back")
        a_y = sem("a_y")
        s_spilled = sem("s_spilled")
        s_staged = sem("s_staged")
        s_scattered = ring("s_scattered")
        s_flags = ring("s_flags")
        s_ea = ring("s_ea")
        s_ea_tail = sem("s_ea_tail")
        s_normed = sem("s_normed")
        s_turned = sem("s_turned")
        s_eaT = sem("s_eaT")
        s_hd = sem("s_hd")
        s_first = sem("s_first")
        s_part = sem("s_part")
        s_part_out = ring("s_part_out")
        s_run0 = sem("s_run0")
        b_gathered = ring("b_gathered")
        b_part = ring("b_part")
        b_normed = sem("b_normed")
        b_turned = sem("b_turned")
        b_hs = sem("b_hs")
        b_lout = ring("b_lout")
        b_first = sem("b_first")
        b_sum = sem("b_sum")
        b_logits = sem("b_logits")
        b_g1 = sem("b_g1")
        b_second = sem("b_second")
        b_g2 = sem("b_g2")
        b_third = sem("b_third")
        b_msg = sem("b_msg")
        s_logits0 = sem("s_logits0")
        s_logits_in = sem("s_logits_in")
        s_logits = sem("s_logits")
        s_edgeT = sem("s_edgeT")
        s_edge_const = sem("s_edge_const")
        s_ladd = sem("s_ladd")
        s_max = sem("s_max")
        s_maxT = sem("s_maxT")
        s_max1 = sem("s_max1")
        s_maxb = sem("s_maxb")
        s_negmax = sem("s_negmax")
        s_exps = sem("s_exps")
        s_sum = sem("s_sum")
        s_inv = sem("s_inv")
        s_turned_exps = sem("s_turned_exps")
        s_exps_in = sem("s_exps_in")
        c_wide = sem("c_wide")
        c_flags = ring("c_flags")
        c_y = ring("c_y")
        c_alpha = sem("c_alpha")
        c_wm = sem("c_wm")
        c_sum = sem("c_sum")
        c_back = sem("c_back")
        c_out = sem("c_out")
        c_scattered = ring("c_scattered")

        def flat(a):
            return a.rearrange("(o n) -> o n", o=1)

        def column(a):
            return a.rearrange("(n o) -> n o", o=1)

        def tile(buf, u, j, width=P):
            return buf[:, u, j * width:(j + 1) * width]

        def last(g):
            return isinstance(g[0], int) and number(g) == LAST

        def segment(n):
            return big[:, bass.ds(n * GE, GE)]

        def take(copy, buf, g, taken, groups=2):
            u = g[1]
            copy(idx_now[:, buf, u:u + groups, :], idx[:, bass.ds(number(g), groups), :]).then_inc(taken, 1)

        def pair_over(eng, taken, g):
            k, u = g
            eng.wait_ge(taken, k * (SLOTS // 2) + (u // 2 + 1))

        def whole(dram, n):
            return dram[bass.ds(n, 1), :, :].rearrange("g p n -> p (g n)")

        block = ctx.enter_context(nc.Block())
        N_W = 19
        DST_PIECE = E // 5
        assert E % DST_PIECE == 0
        COPIES = G - SLOTS
        PIECE = P * (N // (COPIES * P))
        assert (N - COPIES * PIECE) % 8 == 0
        A_GATHERS = 2 * TPG * 16
        GATHERS = TPG * 16

        @block.sync
        def _(sp):
            def rows_in(src, dst, done, src_done):
                for row, a, shift, done in ((dst_row, dst, 0, done), (next_row, dst, 1, done),
                                            (src_row, src, 0, src_done)):
                    mid, end = HALF * P, (TILES - 1) * P
                    sp.dma_start(row[:, 0, :], a[shift:mid + shift].rearrange("(t p) -> t p", p=P)
                                 ).then_inc(done, 16)
                    sp.dma_start(row[0:HALF - 1, 1, :], a[mid + shift:end + shift].rearrange("(t p) -> t p", p=P)
                                 ).then_inc(done, 16)
                    sp.dma_start(row[HALF - 1:HALF, 1, 0:TAIL - shift], flat(a[end + shift:E])).then_inc(done, 16)

            sp.wait_ge(s_fill, 3)
            rows_in(src, dst, s_index, s_index_src)

            def phases(edge_features):
                sp.wait_ge(s_same, 1)
                sp.dma_start(same_dram[:, 0:1], zero_u8[:, :]).then_inc(s_flags_dram, 16)
                for h in range(2):
                    sp.dma_start(same_dram[0, 1 + h * HALF * P:1 + (h + 1) * HALF * P].rearrange("(t p) -> t p", p=P),
                                 same_u8[:, h, :]).then_inc(s_flags_dram, 16)
                sp.wait_ge(s_mirror, 1)
                for h in range(2):
                    sp.dma_start(mirror_dram[0, h * HALF * P:(h + 1) * HALF * P].rearrange("(t p) -> t p", p=P),
                                 mirror_u8[:, h, :]).then_inc(s_flags_dram, 16)
                sp.wait_ge(s_flags_dram, 16 * 5)

                def copy_x(first, rows, b):
                    sp.dma_start(out[bass.ds(first, rows), :].rearrange("(a b) c -> a (b c)", b=b),
                                 x[bass.ds(first, rows), :].rearrange("(a b) c -> a (b c)", b=b)).then_inc(s_copy, 16)

                def edges_in(g, n, done):
                    ends = isinstance(n, int) and n == LAST
                    tiles = TPG - 1 if ends else TPG
                    sp.dma_start(ea[:, g[1], 0:tiles * DE].rearrange("p (j d) -> p j d", d=DE),
                                 edge_features[bass.ds(n * GE, tiles * P), :].rearrange("(j p) d -> p j d", p=P)
                                 ).then_inc(done[g[1]], 16)
                    if ends:
                        sp.dma_start(ea[0:TAIL, g[1], tiles * DE:TPG * DE], edge_features[E - TAIL:E, :]
                                     ).then_inc(s_ea_tail, 16)

                def edges_a(g):
                    over(sp, a_product, ago(g, SLOTS))
                    edges_in(g, number(g), a_ea)

                def flags_a(g):
                    over(sp, a_max, ago(g, SLOTS))
                    sp.dma_start(flags[:, g[1], :], same_dram[:, bass.ds(number(g) * GE, GE)].broadcast_to([P, GE])
                                 ).then_inc(a_flags[g[1]], 16)

                def spill(g):
                    over(sp, a_y, g)
                    sp.dma_start(whole(y_dram, number(g)), segment(number(g))).then_inc(s_spilled, 16)

                def copy_piece(g):
                    copy_x(g[0] * (SLOTS * PIECE) + (g[1] - SLOTS) * PIECE, PIECE, PIECE // P)

                def copy_rest():
                    copy_x(COPIES * PIECE, N - COPIES * PIECE, 8)

                pipeline(sp, G, [(0, flags_a), (0, edges_a), (-SLOTS, copy_piece), (7, spill)], before_drain=copy_rest)

                def inputs_s(g):
                    over(sp, s_hd, ago(g, SLOTS))
                    sp.dma_start(flags[:, g[1], :], mirror_dram[:, bass.ds(number(g) * GE, GE)].broadcast_to([P, GE])
                                 ).then_inc(s_flags[g[1]], 16)
                    over(sp, s_turned, ago(g, SLOTS))
                    edges_in(g, mirrored(g), s_ea)

                def part_out(g):
                    k, u = g
                    over(sp, s_part, g)
                    sp.dma_start(whole(part_dram, mirrored(g)), xd[:, u, :]).then_inc(s_part_out[u], 16)
                    sp.dma_start(logit_dst_dram[:, bass.ds(mirrored(g) * GE, GE)], l_row[:, u, :]
                                 ).then_inc(s_part_out[u], 16)

                all_over(sp, a_max)
                all_over(sp, a_product)
                pipeline(sp, G, [(0, inputs_s), (6, part_out)])

                all_over(sp, s_part_out, 32)
                sp.wait_ge(s_logits0, 1)

                def logits_in(q, dram, done):
                    mid, end = HALF * P, (TILES - 1) * P
                    sp.dma_start(logits[:, q, 0, :], dram[0, 0:mid].rearrange("(t p) -> t p", p=P)).then_inc(done, 16)
                    sp.dma_start(logits[0:HALF - 1, q, 1, :], dram[0, mid:end].rearrange("(t p) -> t p", p=P)
                                 ).then_inc(done, 16)
                    sp.dma_start(logits[HALF - 1:HALF, q, 1, 0:TAIL], dram[:, end:E]).then_inc(done, 16)

                logits_in(0, logit_dst_dram, s_logits_in)

                def part_in(g):
                    over(sp, b_sum, ago(g, SLOTS))
                    sp.dma_start(xd[:, g[1], :], whole(part_dram, number(g))).then_inc(b_part[g[1]], 16)

                def logits_out(g):
                    over(sp, b_logits, g)
                    sp.dma_start(logit_src_dram[:, bass.ds(number(g) * GE, GE)], l_row[:, g[1], :]
                                 ).then_inc(b_lout[g[1]], 16)

                pipeline(sp, G, [(0, part_in), (6, logits_out)])
                all_over(sp, b_lout, 16)
                logits_in(1, logit_src_dram, s_logits_in)

                sp.wait_ge(s_spilled, 16 * G)
                all_over(sp, b_sum)

                def flags_c(g):
                    over(sp, c_sum, ago(g, SLOTS))
                    sp.dma_start(flags[:, g[1], :], same_dram[:, bass.ds(number(g) * GE, GE)].broadcast_to([P, GE])
                                 ).then_inc(c_flags[g[1]], 16)

                def rows_y_c(g):
                    over(sp, c_out, ago(g, SLOTS))
                    sp.dma_start(xd[:, g[1], :], whole(y_dram, number(g))).then_inc(c_y[g[1]], 16)

                pipeline(sp, G, [(0, flags_c), (0, rows_y_c)])

            sp.wait_ge(s_unsorted, 1)
            with sp.If(sp.value_load(unsorted[0:1, 0:1], min_val=0, max_val=EP) > 0):
                for c in range(0, E, DST_PIECE):
                    sp.dma_start(big[:, c:c + DST_PIECE].bitcast(I32),
                                 flat(dst[c:c + DST_PIECE]).broadcast_to([P, DST_PIECE])).then_inc(u_dst_in, 16)
                sp.wait_ge(u_out, 48 * TILES)
                sp.wait_ge(s_index_src, 16 * 3)
                rows_in(src_sorted.rearrange("n o -> (n o)"), dst_sorted.rearrange("n o -> (n o)"), u_index, u_index)
                phases(edge_attr_sorted)
            with sp.Else():
                phases(edge_attr)

        @block.gpsimd
        def _(pool):
            last_row = pool.to_reg(N - 1)
            pool.memset(dst_row[:, :, :], N).then_inc(s_fill, 1)
            pool.memset(next_row[:, :, :], N).then_inc(s_fill, 1)
            pool.memset(src_row[:, :, :], 0).then_inc(s_fill, 1)
            pool.memset(ident[:, :], 0.0)
            pool.memset(flip[:, :], 0.0).then_inc(s_ident0, 1)
            pool.wait_ge(s_ident0, 1)
            pool.affine_select(out=ident[:, :], in_=ident[:, :], compare_op=ALU.not_equal, fill=1.0, base=0,
                               pattern=[[-1, P]], channel_multiplier=1)
            pool.affine_select(out=flip[:, :], in_=flip[:, :], compare_op=ALU.not_equal, fill=1.0,
                               base=-(HALF - 1), pattern=[[1, HALF]], channel_multiplier=1).then_inc(s_ident, 1)
            pool.memset(weT[:, :], 0.0)
            pool.memset(bnode_last[:, :], 0.0).then_inc(s_zeroed, 1)
            pool.memset(logits[:, :, :, :], LOWEST / 4).then_inc(s_logits0, 1)

            def issue(g):
                pool.sem_inc(s_issue, 1)

            def at(u, table, j):
                c = table * TPG + j
                return bass.IndirectOffsetOnAxis(ap=idx_now[:, table // 2, u, c:c + 1], axis=0)

            def gather(u, buf, table, rows, done):
                for j in range(TPG):
                    pool.indirect_dma_start(tile(buf, u, j), None, rows, at(u, table, j),
                                            bounds_check=last_row, oob_is_err=False).then_inc(done[u], 16)

            def scatter(u, done):
                for j in range(TPG):
                    pool.indirect_dma_start(out, at(u, 2, j), tile(y_out, u, j), None,
                                            bounds_check=last_row, oob_is_err=False).then_inc(done[u], 16)

            last_edge = pool.to_reg(EP - 1)
            pool.wait_ge(s_unsorted, 1)
            with pool.If(pool.value_load(unsorted[0:1, 0:1], min_val=0, max_val=EP) > 0):
                pool.memset(lower[:, :], 1.0).then_inc(u_lower0, 1)
                pool.wait_ge(u_lower0, 1)
                pool.affine_select(out=lower[:, :], in_=lower[:, :], compare_op=ALU.is_gt, fill=0.0, base=0,
                                   pattern=[[-1, P]], channel_multiplier=1).then_inc(u_lower, 1)
                pool.wait_ge(u_ranked, 1)

                def place(t, rows):
                    pool.dma_start(ea[0:rows, 0, 0:DE], edge_attr[bass.ds(t * P, rows), :]).then_inc(u_in, 16)
                    pool.dma_start(src_now[0:rows, :], column(src[bass.ds(t * P, rows)])).then_inc(u_in, 16)
                    pool.dma_start(dst_now[0:rows, :], column(dst[bass.ds(t * P, rows)])).then_inc(u_in, 16)
                    pool.tensor_copy(rank_now[:, :], ranks[:, bass.ds(t, 1)]).then_inc(u_taken, 1)
                    pool.wait_ge(u_taken, t + 1)
                    pool.wait_ge(u_in, t * 48 + 48)
                    pool.sem_inc(s_issue, 1)
                    for buf, dram in ((ea[:, 0, 0:DE], edge_attr_sorted), (src_now[:, :], src_sorted),
                                      (dst_now[:, :], dst_sorted)):
                        pool.indirect_dma_start(dram, bass.IndirectOffsetOnAxis(ap=rank_now[:, 0:1], axis=0), buf,
                                                None, bounds_check=last_edge, oob_is_err=False
                                                ).then_inc(u_out, 16)
                    pool.wait_ge(u_out, t * 48 + 48)
                    pool.sem_inc(s_issue, 1)

                with pool.Fori(0, TILES - 1) as t:
                    place(t, P)
                place(TILES - 1, TAIL)

            def gather_a(g):
                over(pool, a_normed, ago(g, SLOTS))
                over(pool, a_copied, ago(g, SLOTS))
                pair_over(pool, a_rows, g)
                issue(g)
                gather(g[1], xs, 0, x, a_gathered)
                gather(g[1], xd, 1, x, a_gathered)

            pipeline(pool, G, [(0, gather_a)])

            pool.wait_ge(s_copy, 16 * (COPIES + 1))

            def scatter_s(g):
                over(pool, s_staged, g)
                pair_over(pool, s_rows, g)
                issue(g)
                scatter(g[1], s_scattered)

            pipeline(pool, G, [(0, scatter_s)])

            all_over(pool, s_scattered, GATHERS)
            all_over(pool, a_normed)

            def gather_b(g):
                over(pool, b_normed, ago(g, SLOTS))
                pair_over(pool, b_rows, g)
                issue(g)
                gather(g[1], xs, 0, out, b_gathered)

            pipeline(pool, G, [(0, gather_b)])

            def scatter_c(g):
                over(pool, c_out, g)
                pair_over(pool, c_rows, g)
                issue(g)
                scatter(g[1], c_scattered)

            pipeline(pool, G, [(0, scatter_c)])
            all_over(pool, c_scattered, GATHERS)

        @block.vector
        def _(dve):
            st = Steps(dve, s_dve)
            dve.memset(zero_u8[:, :], 0)
            dve.memset(one_last[:, :], 0.0)
            dve.memset(eaT[DE:DE + 1, :, :], 1.0).then_inc(s_eaT_ones, 1)
            dve.memset(ones[:, :], 1.0).then_inc(s_ones, 1)
            dve.memset(run[:, 1, GE - 1:GE], 0.0)
            dve.memset(hd[:, 1, 0:1], 0.0).then_inc(s_run0, 1)

            dve.wait_ge(s_index, 16 * 6)
            st.inc(dve.tensor_tensor(mirror_row[:, :, :], dst_row[:, :, :], next_row[:, :, :], ALU.is_gt))
            st.wait()
            dve.tensor_reduce(descents[:, :], mirror_row[:, :, :].rearrange("t h p -> t (h p)"), AX_X, ALU.add
                              ).then_inc(s_descents, 1)
            dve.wait_ge(s_descents_sum, 1)
            dve.tensor_copy(unsorted[:, :], bank[6][0:1, 0:1]).then_inc(s_unsorted, 1)
            dve.wait_ge(s_unsorted, 1)
            with dve.If(dve.value_load(unsorted[0:1, 0:1], min_val=0, max_val=EP) > 0):
                ut = Steps(dve, u_step)
                dve.wait_ge(u_dst_in, 16 * (E // DST_PIECE))
                dve.memset(big[:, E:EP], float(N))
                ut.inc(dve.tensor_copy(big[:, 0:E], big[:, 0:E].bitcast(I32)))
                dve.wait_ge(s_ident, 1)
                dve.wait_ge(u_lower, 1)
                QUARTER = EP // 4
                with dve.Fori(0, TILES) as t:
                    ut.enter(t, 10)
                    here = big[:, bass.ds(t * P, P)]
                    ut.wait()
                    ut.inc(dve.tensor_tensor(square[:, :], here, ident[:, :], ALU.mult))
                    ut.wait()
                    ut.inc(dve.tensor_reduce(own[:, :], square[:, :], AX_X, ALU.add))
                    ut.wait()
                    for q in range(4):
                        ut.inc(dve.tensor_scalar(below[:, :], big[:, q * QUARTER:(q + 1) * QUARTER], own[:, 0:1],
                                                 0.0, ALU.is_lt, ALU.add, accum_out=counts[:, q:q + 1]))
                        ut.wait()
                    ut.inc(dve.scalar_tensor_tensor(out=square[:, :], in0=here, scalar=own[:, 0:1],
                                                    in1=lower[:, :], op0=ALU.is_equal, op1=ALU.mult))
                    ut.wait()
                    ut.inc(dve.tensor_reduce(counts[:, 4:5], square[:, :], AX_X, ALU.add))
                    ut.wait()
                    ut.inc(dve.tensor_reduce(counts[:, 5:6], counts[:, 0:5], AX_X, ALU.add))
                    ut.wait()
                    dve.tensor_copy(ranks[:, bass.ds(t, 1)], counts[:, 5:6])
                    ut.inc(dve.tensor_scalar(here, here, -0.5, None, ALU.add))
                ut.leave(TILES)
                ut.wait()
                dve.sem_inc(u_ranked, 1)
                dve.wait_ge(u_index, 16 * 9)
                dve.sem_inc(s_link, 1)

            dve.wait_ge(s_index_src, 16 * 3)
            st.inc(dve.tensor_tensor(same_row[:, :, :], dst_row[:, :, :], next_row[:, :, :], ALU.is_equal))
            dve.tensor_copy(idx_row[:, 0, :, :], src_row[:, :, :])
            dve.tensor_scalar(idx_row[:, 1, :, :], dst_row[:, :, :], float(N - 1), None, ALU.min)
            st.wait()
            dve.scalar_tensor_tensor(out=idx_row[:, 2, :, :], in0=same_row[:, :, :], scalar=float(SKIP),
                                     in1=dst_row[:, :, :], op0=ALU.mult, op1=ALU.add).then_inc(s_idx_rows, 1)
            dve.tensor_copy(same_u8[:, :, :], same_row[:, :, :]).then_inc(s_same, 1)
            for h in range(2):
                ins = dve.tensor_copy(mirror_row[:, h, :], same_row[:, h, ::-1])
            ins.then_inc(s_mirrored, 1)
            dve.memset(idx[:, G, :], 0)
            dve.wait_ge(s_idxT, 1)
            for table in range(3):
                dve.tensor_copy(idx[:, 0:G, table * TPG:(table + 1) * TPG],
                                bank[table][:, 0:TILES].rearrange("p (g j) -> p g j", j=TPG))
            dve.tensor_scalar(is_last[:, :, :], bank[2][:, 0:TILES].rearrange("p (g j) -> p g j", j=TPG),
                              float(SKIP), None, ALU.is_lt).then_inc(s_idx, 1)
            dve.wait_ge(s_idx, 1)
            for u in range(0, SLOTS, 2):
                take(dve.tensor_copy, 0, (0, u), a_rows)
            for h in range(2):
                ins = dve.tensor_copy(mirror_u8[:, 1 - h, :], bank[3][0:HALF, h * P:(h + 1) * P])
            ins.then_inc(s_mirror, 1)

            dve.wait_ge(s_weights, 16 * N_W)
            dve.wait_ge(s_eaT_ones, 1)
            dve.memset(one_last[:, DE:DE + 1], 1.0)
            dve.tensor_tensor(w0_dst[:, :], w0_dst[:, :], w0_src[:, :], ALU.subtract).then_inc(s_wdiff, 1)
            dve.wait_ge(s_wT, 1)
            dve.tensor_copy(wnT[:, :], bank[4][:, 0:P])
            dve.tensor_copy(weT[:, 0:DE], bank[5][:, 0:DE]).then_inc(s_wT_in, 1)
            dve.wait_ge(s_u, 1)
            dve.tensor_copy(u_src[:, :], bank[6][:, 0:1])
            dve.tensor_copy(u_dst[:, :], bank[6][:, 1:2])
            dve.tensor_copy(u_edge[:, :], bank[7][:, 0:DE + 1]).then_inc(s_u_in, 1)

            LN_LINKS = 10

            def stats(g, tiles):
                for j, t in enumerate(tiles):
                    ins = dve.bn_stats(bst[:, g[1] % 2, j, :], t)
                st.inc(ins)

            def norm_links(slots, m, mask_of=None):
                n0, q = st.n, len(slots)
                st.wait()
                dve.sem_inc(s_link, 1)
                for u in slots:
                    for j in range(m):
                        ins = dve.bn_aggr(mv[:, u, j, :], bst[:, u % 2, j, :])
                st.inc(ins)
                yield
                u0 = slots[0]
                v, y, t, w = var[:, 0:q, 0:m], rstd[:, u0:u0 + q, 0:m], newton[:, 0, 0:q, 0:m], newton[:, 1, 0:q, 0:m]
                st.wait()
                st.inc(dve.tensor_scalar(v, mv[:, u0:u0 + q, 0:m, 1], EPS, None, ALU.add))
                yield
                st.wait()
                st.inc(dve.tensor_scalar(y.bitcast(I32), v.bitcast(I32), -0.5, float(RSQRT_SEED), ALU.mult, ALU.add))
                yield
                st.wait()
                dve.tensor_scalar(w, y, 0.375, None, ALU.mult)
                st.inc(dve.tensor_tensor(t, y, y, ALU.mult))
                yield
                st.wait()
                st.inc(dve.tensor_tensor(t, t, v, ALU.mult))
                yield
                st.wait()
                st.inc(dve.scalar_tensor_tensor(out=t, in0=t, scalar=-10.0 / 3, in1=t, op0=ALU.add, op1=ALU.mult))
                yield
                st.wait()
                st.inc(dve.scalar_tensor_tensor(out=y, in0=t, scalar=5.0, in1=w, op0=ALU.add, op1=ALU.mult))
                yield
                st.wait()
                st.inc(dve.scalar_tensor_tensor(out=t, in0=y, scalar=-0.5, in1=y, op0=ALU.mult, op1=ALU.mult))
                yield
                st.wait()
                if mask_of is not None:
                    for u in slots:
                        dve.tensor_tensor(rstd[:, u, 0:m], rstd[:, u, 0:m], mask_of(u), ALU.mult)
                st.inc(dve.tensor_tensor(t, t, v, ALU.mult))
                yield
                st.wait()
                st.inc(dve.scalar_tensor_tensor(out=y, in0=t, scalar=1.5, in1=y, op0=ALU.add, op1=ALU.mult))
                yield
                assert st.n - n0 == LN_LINKS, st.n - n0

            LN_STEPS = SLOTS + SLOTS // 2 * LN_LINKS

            def norms(g, live, tiles_of, m, mask_of=None):
                if live(0):
                    stats(g, tiles_of(g))
                if g[1] % 2 and live(1):
                    slots = [g[1] - 1, g[1]] if live(0) else [g[1] - 1]
                    return norm_links(slots, m, mask_of and (lambda u: mask_of(g if u == g[1] else ago(g, 1))))
                return iter(())

            def applies(g, tiles_of, turned, normed):
                u, tiles = g[1], tiles_of(g)
                over(dve, turned, ago(g, 2))
                for j, t in enumerate(tiles):
                    ins = dve.tensor_scalar(tile(xn, u % 2, j), t, mv[:, u, j, 0:1], rstd[:, u, j:j + 1],
                                            ALU.subtract, ALU.mult)
                    if j == len(tiles) - 1:
                        ins.then_inc(normed, 1)
                    yield

            def tiles_a(g):
                return [tile(buf, g[1], j) for buf in (xs, xd) for j in range(TPG)]

            def max_a(g):
                u, d = g[1], g[1] % 2
                over(dve, a_biased, g)
                over(dve, a_flags, g, 16)
                over(dve, a_back, ago(g, 2))
                over(dve, a_max, ago(g, 1))
                dve.tensor_tensor_scan(run[:, d, :], flags[:, u, :], m_a[:, d, :], run[:, 1 - d, GE - 1:GE],
                                       ALU.mult, ALU.max).then_inc(a_max, 1)

            def add_y(g):
                over(dve, a_back, g)
                over(dve, a_copied, g)
                dve.tensor_tensor(segment(number(g)), bank[6 + g[1] % 2][:, :], segment(number(g)), ALU.add
                                  ).then_inc(a_y, 1)

            def edge_product(g):
                over(dve, a_ea, g, 16)
                if last(g):
                    dve.wait_ge(s_ea_tail, 16)
                over(dve, a_edge, ago(g, 1))
                dve.tensor_tensor(product[:, :, :], ea[:, g[1], :].rearrange("p (j d) -> p j d", d=DE),
                                  u_edge[:, 0:DE].rearrange("p (j d) -> p j d", j=1).broadcast_to([P, TPG, DE]),
                                  ALU.mult).then_inc(a_product, 1)

            def edge_logits(g):
                over(dve, a_product, g)
                dve.tensor_reduce(logits_edge[:, bass.ds(number(g) * TPG, TPG)], product[:, :, :], AX_X, ALU.add
                                  ).then_inc(a_edge, 1)

            def step_a(g, live):
                if live(2):
                    st.wait()
                    for _ in applies(ago(g, 2), tiles_a, a_turned, a_normed):
                        pass
                if live(0):
                    over(dve, a_gathered, g, A_GATHERS)
                if g[1] % 2 and live(-3):
                    take(dve.tensor_copy, 0, ago(g, -3), a_rows)
                chain = norms(g, live, tiles_a, 2 * TPG)
                next(chain, None)
                for lag, stage in ((4, edge_product), (4, max_a), (4, edge_logits), (5, add_y)):
                    if live(lag):
                        stage(ago(g, lag))
                    next(chain, None)
                for _ in chain:
                    pass

            dve.wait_ge(s_run0, 1)
            in_steps(dve, G, 5, step_a, st, LN_STEPS, ahead=3)
            for u in range(0, SLOTS, 2):
                take(dve.tensor_copy, 0, (0, u), b_rows)

            def tiles_s(g):
                return [big[:, bass.ds(mirrored(g) * GE + j * P, P)] for j in range(TPG)]

            def spread_s(g):
                u, d = g[1], g[1] % 2
                over(dve, s_turned, g)
                over(dve, s_flags, g, 16)
                over(dve, s_first, ago(g, 2))
                over(dve, s_hd, ago(g, 1))
                dve.tensor_tensor_scan(hd[:, d, ::-1], flags[:, u, :], bank[d][:, ::-1],
                                       hd[:, 1 - d, 0:1], ALU.mult, ALU.max).then_inc(s_hd, 1)

            def last_of(g):
                return is_last[:, bass.ds(mirrored(g), 1), :].rearrange("p g j -> p (g j)")

            def step_s(g, live):
                chain = norms(g, live, tiles_s, TPG, last_of)
                next(chain, None)
                if live(2):
                    if not (g[1] % 2 and live(1)):
                        st.wait(1 if live(0) else 0)
                    for _ in applies(ago(g, 2), tiles_s, s_turned, s_normed):
                        next(chain, None)
                if live(3):
                    spread_s(ago(g, 3))
                for _ in chain:
                    pass

            all_over(dve, a_y)
            all_over(dve, a_msg)
            dve.memset(hd[:, 1, 0:1], 0.0).then_inc(s_run0, 1)
            dve.wait_ge(s_run0, 2)
            in_steps(dve, G, 3, step_s, st, LN_STEPS)

            def tiles_b(g):
                return [tile(xs, g[1], j) for j in range(TPG)]

            def sum_b(g):
                u, d = g[1], g[1] % 2
                over(dve, b_first, g)
                over(dve, b_part, g, 16)
                over(dve, b_g1, ago(g, 2))
                dve.tensor_tensor(hd[:, d, :], bank[2 + d][:, :], xd[:, u, :], ALU.add).then_inc(b_sum, 1)

            def step_b(g, live):
                if live(2):
                    st.wait()
                    for _ in applies(ago(g, 2), tiles_b, b_turned, b_normed):
                        pass
                if live(0):
                    over(dve, b_gathered, g, GATHERS)
                if g[1] % 2 and live(-3):
                    take(dve.tensor_copy, 0, ago(g, -3), b_rows)
                chain = norms(g, live, tiles_b, TPG)
                next(chain, None)
                if live(4):
                    sum_b(ago(g, 4))
                for _ in chain:
                    pass

            def add_edge():
                dve.wait_ge(s_logits_in, 16 * 3)
                dve.wait_ge(s_edge_const, 1)
                dve.tensor_tensor(logits[:, 0, :, :], logits[:, 0, :, :], edge_rows[:, :, :], ALU.add
                                  ).then_inc(s_logits, 1)

            all_over(dve, s_first)
            dve.wait_ge(s_edgeT, 1)
            dve.tensor_scalar(edge_rows[:, :, :].rearrange("t h p -> t (h p)"), bank[7][0:HALF, 0:2 * P],
                              u_edge[0:HALF, DE:DE + 1], None, ALU.add).then_inc(s_edge_const, 1)
            in_steps(dve, G, 4, step_b, st, LN_STEPS, ahead=3, before_drain=add_edge)

            dve.wait_ge(s_logits_in, 16 * 6)
            dve.wait_ge(s_logits, 1)
            dve.tensor_tensor(logits[:, 0, :, :], logits[:, 0, :, :], logits[:, 1, :, :], ALU.add
                              ).then_inc(s_ladd, 1)
            dve.wait_ge(s_ladd, 1)
            dve.tensor_reduce(sm[0:HALF, 0:1], logits[:, 0, :, :].rearrange("t h p -> t (h p)"), AX_X, ALU.max
                              ).then_inc(s_max, 1)
            dve.wait_ge(s_maxT, 1)
            dve.tensor_reduce(mrow[:, 0:1], bank[0][0:1, 0:HALF], AX_X, ALU.max).then_inc(s_max1, 1)
            dve.wait_ge(s_maxb, 1)
            dve.tensor_scalar(sm[:, 1:2], bank[1][:, 0:1], -1.0, None, ALU.mult).then_inc(s_negmax, 1)
            dve.wait_ge(s_sum, 1)
            dve.reciprocal(sm[:, 3:4], bank[2][:, 0:1]).then_inc(s_inv, 1)
            dve.wait_ge(s_turned_exps, 1)
            dve.tensor_copy(weights[:, :], bank[3][:, 0:TILES]).then_inc(s_exps_in, 1)
            all_over(dve, b_third)
            dve.memset(run[:, 1, GE - 1:GE], 0.0).then_inc(s_run0, 1)
            dve.wait_ge(s_run0, 3)

            def weigh(g):
                u, d = g[1], g[1] % 2
                over(dve, c_alpha, g)
                over(dve, c_sum, ago(g, 2))
                dve.tensor_tensor(hd[:, d, :], segment(number(g)), bank[d][:, :], ALU.mult).then_inc(c_wm, 1)

            def sum_c(g):
                u, d = g[1], g[1] % 2
                over(dve, c_wm, g)
                over(dve, c_flags, g, 16)
                over(dve, c_back, ago(g, 2))
                over(dve, c_sum, ago(g, 1))
                dve.tensor_tensor_scan(run[:, d, :], flags[:, u, :], hd[:, d, :], run[:, 1 - d, GE - 1:GE],
                                       ALU.mult, ALU.add).then_inc(c_sum, 1)

            def add_out(g):
                u, d = g[1], g[1] % 2
                over(dve, c_back, g)
                over(dve, c_y, g, 16)
                over(dve, c_scattered, ago(g, SLOTS), GATHERS)
                if not (isinstance(g[0], int) and g[0] == 0):
                    if u % 2:
                        take(dve.tensor_copy, 1, ago(g, 1), c_rows)
                    elif last(g):
                        take(dve.tensor_copy, 1, g, c_rows, 1)
                dve.tensor_tensor(y_out[:, u, :], bank[6 + d][:, :], xd[:, u, :], ALU.add).then_inc(c_out, 1)

            all_over(dve, b_msg)
            all_over(dve, s_scattered, GATHERS)
            for v in range(0, SLOTS, 2):
                take(dve.tensor_copy, 1, (0, v), c_rows)
            pipeline(dve, G, [(1, weigh), (2, sum_c), (4, add_out)])

        @block.tensor
        def _(pe):
            def turn(dest, source, rows=P):
                for j in range(TPG):
                    ins = pe.transpose(dest[0:rows, j * P:(j + 1) * P], source(j), ident[:, :])
                return ins

            pe.wait_ge(s_ones, 1)
            pe.wait_ge(s_descents, 1)
            pe.matmul(bank[6][0:1, 0:1], descents[:, :], ones[0:HALF, 0:1], start=True, stop=True
                      ).then_inc(s_descents_sum, 1)

            pe.wait_ge(s_ident, 1)
            pe.wait_ge(s_idx_rows, 1)
            for table in range(3):
                for h in range(2):
                    ins = pe.transpose(bank[table][:, h * HALF:(h + 1) * HALF], idx_row[:, table, h, :],
                                       ident[0:HALF, 0:HALF])
            pe.wait_ge(s_mirrored, 1)
            for h in range(2):
                ins = pe.matmul(bank[3][0:HALF, h * P:(h + 1) * P], flip[:, :], mirror_row[:, h, :],
                                start=True, stop=True)
            ins.then_inc(s_idxT, 1)
            pe.wait_ge(s_weights, 16 * N_W)
            pe.transpose(bank[4][:, 0:P], wn[:, :], ident[:, :])
            pe.transpose(bank[5][:, 0:DE], we[:, :], ident[0:DE, 0:DE]).then_inc(s_wT, 1)
            pe.wait_ge(s_wdiff, 1)
            pe.wait_ge(s_wT_in, 1)
            pe.matmul(bank[6][:, 0:1], wnT[:, :], watt[:, 0:1], start=True, stop=True)
            pe.matmul(bank[6][:, 1:2], wnT[:, :], watt[:, 1:2], start=True, stop=True)
            for k, (w_att, columns) in enumerate(((watt[:, 2:3], weT), (watt[:, 0:1], bnode_last),
                                                  (watt[:, 1:2], bnode_last), (batt[:, :], one_last))):
                ins = pe.matmul(bank[7][:, 0:DE + 1], w_att.broadcast_to([w_att.shape[0], P]), columns[:, :],
                                start=k == 0, stop=k == 3)
            ins.then_inc(s_u, 1)
            pe.wait_ge(s_u_in, 1)

            def turn_a(g):
                d = g[1] % 2
                over(pe, a_normed, g)
                over(pe, a_relu, ago(g, 2))
                turn(bank[d], lambda j: tile(xn, d, j))
                turn(bank[2 + d], lambda j: tile(xn, d, TPG + j)).then_inc(a_turned, 1)

            def messages_a(g):
                d = g[1] % 2
                over(pe, a_relu, g)
                over(pe, a_biased, ago(g, 2))
                pe.matmul(bank[4 + d][:, :], w0_src[:, :], hs[:, d, :], start=True, stop=False)
                pe.matmul(bank[4 + d][:, :], w0_dst[:, :], hd[:, d, :], start=False, stop=True
                          ).then_inc(a_msg, 1)

            def back_a(g):
                d = g[1] % 2
                over(pe, a_max, g)
                over(pe, a_y, ago(g, 2))
                turn(bank[6 + d], lambda j: tile(run, d, j)).then_inc(a_back, 1)

            pipeline(pe, G, [(1, turn_a), (2, messages_a), (3, back_a)])

            def turn_s(g):
                u, d = g[1], g[1] % 2
                over(pe, s_normed, g)
                over(pe, s_ea, g, 16)
                over(pe, s_hd, ago(g, 2))
                over(pe, s_eaT, ago(g, 2))
                turn(bank[d], lambda j: tile(xn, d, j))
                turn(bank[2 + d], lambda j: tile(ea, u, j, DE), DE).then_inc(s_turned, 1)

            def first_s(g):
                u, d = g[1], g[1] % 2
                over(pe, s_hd, g)
                over(pe, s_eaT, g)
                over(pe, s_part, ago(g, 2))
                pe.matmul(bank[4 + d][:, :], w1_edge[:, :], eaT[:, d, :], start=True, stop=False)
                pe.matmul(bank[4 + d][:, :], w1_dst[:, :], hd[:, d, :], start=False, stop=True)
                ins = pe.matmul(bank[6 + d][0:1, :], u_dst[:, :], hd[:, d, :], start=True, stop=True)
                ins.then_inc(s_first, 1)

            all_over(pe, a_y)
            pe.wait_ge(s_ea_tail, 32)
            pipeline(pe, G, [(1, turn_s), (3, first_s)])

            def turn_b(g):
                d = g[1] % 2
                over(pe, b_normed, g)
                over(pe, b_hs, ago(g, 2))
                turn(bank[d], lambda j: tile(xn, d, j)).then_inc(b_turned, 1)

            def first_b(g):
                d = g[1] % 2
                over(pe, b_hs, g)
                over(pe, b_sum, ago(g, 2))
                over(pe, b_logits, ago(g, 2))
                pe.matmul(bank[2 + d][:, :], w1_src[:, :], hs[:, d, :], start=True, stop=True)
                pe.matmul(bank[4 + d][0:1, :], u_src[:, :], hs[:, d, :], start=True, stop=True
                          ).then_inc(b_first, 1)

            def second_b(g):
                over(pe, b_g1, g)
                over(pe, b_g2, ago(g, 1))
                pe.matmul(bank[6][:, :], w2[:, :], m_a[:, g[1] % 2, :], start=True, stop=True
                          ).then_inc(b_second, 1)

            def third_b(g):
                over(pe, b_g2, g)
                if isinstance(g[0], int) and number(g) == 0:
                    pe.wait_ge(s_edge_const, 1)
                over(pe, b_msg, ago(g, 1))
                pe.matmul(bank[7][:, :], w3[:, :], run[:, g[1] % 2, :], start=True, stop=True
                          ).then_inc(b_third, 1)

            all_over(pe, s_part)
            for h in range(2):
                ins = pe.transpose(bank[7][0:HALF, h * P:(h + 1) * P], logits_edge[:, h * HALF:(h + 1) * HALF],
                                   ident[:, :])
            ins.then_inc(s_edgeT, 1)
            def step_b(g, live):
                for lag, stage in ((1, turn_b), (2, first_b), (4, second_b), (5, third_b)):
                    if live(lag):
                        stage(ago(g, lag))
                if live(5) and not live(4):
                    pe.wait_ge(s_max, 1)
                    all_over(pe, b_hs)
                    pe.transpose(bank[0][0:1, 0:HALF], sm[0:HALF, 0:1], ident[0:HALF, 0:HALF]).then_inc(s_maxT, 1)
                if live(6) and not live(5):
                    pe.wait_ge(s_max1, 1)
                    pe.matmul(bank[1][:, 0:1], ones[0:1, :], mrow[:, 0:1], start=True, stop=True
                              ).then_inc(s_maxb, 1)

            in_steps(pe, G, 6, step_b)

            pe.wait_ge(s_exps, 1)
            all_over(pe, b_sum)
            pe.matmul(bank[2][:, 0:1], ones[0:HALF, :], sm[0:HALF, 2:3], start=True, stop=True).then_inc(s_sum, 1)
            for h in range(2):
                ins = pe.transpose(bank[3][:, h * HALF:(h + 1) * HALF], logits[:, 1, h, :], ident[0:HALF, 0:HALF])
            ins.then_inc(s_turned_exps, 1)

            def spread_c(g):
                d = g[1] % 2
                over(pe, c_wide, g)
                over(pe, c_wm, ago(g, 2))
                turn(bank[d], lambda j: tile(m_a, d, j)).then_inc(c_alpha, 1)

            def back_c(g):
                d = g[1] % 2
                over(pe, c_sum, g)
                over(pe, c_out, ago(g, 2))
                turn(bank[6 + d], lambda j: tile(run, d, j)).then_inc(c_back, 1)

            all_over(pe, b_msg)
            pipeline(pe, G, [(0, spread_c), (2, back_c)])

        @block.scalar
        def _(act):
            act.wait_ge(s_index, 16 * 6)
            act.wait_ge(s_index_src, 16 * 3)
            for dest, a in ((w0_dst[:, :], W0[0:C, :]), (w0_src[:, :], W0[C:2 * C, :]),
                            (w1_src[:, :], W_m1[0:C, :]), (w1_dst[:, :], W_m1[C:2 * C, :]),
                            (w1_edge[0:DE, :], W_m1[2 * C:2 * C + DE, :]), (w1_edge[DE:DE + 1, :], flat(b_m1)),
                            (w2[:, :], W_m2), (w3[:, :], W_m3), (wn[:, :], W_node), (we[:, :], W_edge),
                            (col[:, 0:1], column(b0)), (col[:, 1:2], column(b_m2)), (col[:, 2:3], column(b_m3)),
                            (watt[:, 0:1], W_att[0:P, :]), (watt[:, 1:2], W_att[P:2 * P, :]),
                            (watt[:, 2:3], W_att[2 * P:3 * P, :]), (batt[:, :], flat(b_att))):
                act.dma_start(dest, a).then_inc(s_weights, 16)
            act.wait_ge(s_zeroed, 1)
            act.dma_start(bnode_last[:, DE:DE + 1], column(b_node)).then_inc(s_weights, 16)
            act.dma_start(weT[:, DE:DE + 1], column(b_edge)).then_inc(s_weights, 16)

            def copy_a(g):
                over(act, a_gathered, g, A_GATHERS)
                act.activation(segment(number(g)), xd[:, g[1], :], ACT.Copy).then_inc(a_copied, 1)

            def relu_a(g):
                d = g[1] % 2
                over(act, a_turned, g)
                over(act, a_msg, ago(g, 2))
                act.activation(hs[:, d, :], bank[d][:, :], ACT.Relu)
                act.activation(hd[:, d, :], bank[2 + d][:, :], ACT.Relu).then_inc(a_relu, 1)

            def bias_a(g):
                d = g[1] % 2
                over(act, a_msg, g)
                over(act, a_max, ago(g, 2))
                act.activation(m_a[:, d, :], bank[4 + d][:, :], ACT.Identity, bias=col[:, 0:1]
                               ).then_inc(a_biased, 1)

            act.wait_ge(s_weights, 16 * N_W)
            act.wait_ge(s_run0, 1)
            def copy_rows(dest, rows):
                return act.activation(dest, rows, ACT.Copy)

            def stage_s(g):
                over(act, a_y, g)
                over(act, s_scattered, ago(g, SLOTS), GATHERS)
                if g[1] % 2:
                    take(copy_rows, 1, ago(g, 1), s_rows)
                elif last(g):
                    take(copy_rows, 1, g, s_rows, 1)
                act.activation(y_out[:, g[1], :], segment(number(g)), ACT.Copy).then_inc(s_staged, 1)

            def first_stages():
                for u in range(SLOTS):
                    stage_s((0, u))

            pipeline(act, G, [(0, copy_a), (1, relu_a), (2, bias_a)], ahead=4, before_drain=first_stages)

            def edge_s(g):
                d = g[1] % 2
                over(act, s_turned, g)
                over(act, s_first, ago(g, 2))
                act.activation(eaT[0:DE, d, :], bank[2 + d][0:DE, :], ACT.Copy).then_inc(s_eaT, 1)

            def part_s(g):
                u, d = g[1], g[1] % 2
                over(act, s_first, g)
                over(act, s_part_out, ago(g, SLOTS), 32)
                act.activation(xd[:, u, :], bank[4 + d][:, :], ACT.Copy)
                act.activation(l_row[:, u, :], bank[6 + d][0:1, :], ACT.Copy).then_inc(s_part, 1)

            pipeline(act, G, [(-SLOTS, stage_s), (2, edge_s), (4, part_s)], ahead=SLOTS + 1)

            def relu_b(g):
                d = g[1] % 2
                over(act, b_turned, g)
                over(act, b_first, ago(g, 2))
                act.activation(hs[:, d, :], bank[d][:, :], ACT.Relu).then_inc(b_hs, 1)

            def logits_b(g):
                u, d = g[1], g[1] % 2
                over(act, b_first, g)
                over(act, b_lout, ago(g, SLOTS), 16)
                act.activation(l_row[:, u, :], bank[4 + d][0:1, :], ACT.Copy).then_inc(b_logits, 1)

            def gelu1_b(g):
                d = g[1] % 2
                over(act, b_sum, g)
                over(act, b_second, ago(g, 2))
                act.activation(m_a[:, d, :], hd[:, d, :], ACT.Gelu_apprx_tanh).then_inc(b_g1, 1)

            def gelu2_b(g):
                d = g[1] % 2
                over(act, b_second, g)
                over(act, b_third, ago(g, 2))
                act.activation(run[:, d, :], bank[6][:, :], ACT.Gelu_apprx_tanh, bias=col[:, 1:2]
                               ).then_inc(b_g2, 1)

            def exponentials():
                act.wait_ge(s_negmax, 1)
                act.activation(logits[:, 1, :, :].rearrange("t h p -> t (h p)"),
                               logits[:, 0, :, :].rearrange("t h p -> t (h p)"), ACT.Exp,
                               bias=sm[0:HALF, 1:2], accum_out=sm[0:HALF, 2:3]).then_inc(s_exps, 1)

            def message_b(g):
                if last(g):
                    exponentials()
                over(act, b_third, g)
                act.activation(segment(number(g)), bank[7][:, :], ACT.Identity, bias=col[:, 2:3]
                               ).then_inc(b_msg, 1)

            all_over(act, s_staged)
            all_over(act, s_normed)
            all_over(act, s_part_out, 32)
            act.wait_ge(s_spilled, 16 * G)
            pipeline(act, G, [(1, relu_b), (2, logits_b), (3, gelu1_b), (4, gelu2_b), (5, message_b)])

            def wide_c(g):
                d = g[1] % 2
                over(act, c_alpha, ago(g, 2))
                act.activation(m_a[:, d, :].rearrange("p (j c) -> p j c", c=P),
                               weights[:, bass.ds(number(g) * TPG, TPG)].rearrange("p (j c) -> p j c", c=1)
                               .broadcast_to([P, TPG, P]), ACT.Identity, scale=sm[:, 3:4]).then_inc(c_wide, 1)

            act.wait_ge(s_inv, 1)
            act.wait_ge(s_exps_in, 1)
            all_over(act, b_second)
            pipeline(act, G, [(0, wide_c)])


_INS = ['x', 'src', 'dst', 'edge_attr_64', 'L0_gnn_W', 'L0_gnn_b', 'L1_gnn_W_node', 'L1_gnn_b_node',
        'L1_gnn_W_edge', 'L1_gnn_b_edge', 'L1_gnn_W_att', 'L1_gnn_b_att', 'L1_gnn_W_m1', 'L1_gnn_b_m1',
        'L1_gnn_W_m2', 'L1_gnn_b_m2', 'L1_gnn_W_m3', 'L1_gnn_b_m3']


def kernel(**inputs):
    import numpy as _np
    import concourse.bacc as _bacc
    from concourse import mybir as _mybir
    from concourse.bass_utils import run_bass_kernel_spmd as _run

    nc = _bacc.Bacc("TRN2", target_bir_lowering=False, num_devices=1)
    arrays, args = {}, []
    for name in _INS:
        a = _np.ascontiguousarray(inputs[name])
        arrays[f"in_{name}_dram"] = a
        args.append(nc.dram_tensor(f"in_{name}_dram", a.shape, _mybir.dt.from_np(a.dtype), kind="ExternalInput").ap())
    shape = tuple(inputs["x"].shape)
    out = nc.dram_tensor("out_0_dram", shape, _mybir.dt.float32, kind="ExternalOutput").ap()
    gnn_kernel(nc, *args, out)
    r = _run(nc, [arrays], core_ids=[0])
    return r.results[0]["out_0_dram"]
```
